# Optimizing a Trainium2 kernel written in Bass

```python
import numpy as np
import jax
import jax.numpy as jnp

def _softmax(x, axis=-1):
    return jax.nn.softmax(x, axis=axis)

def _gelu(x):
    return jax.nn.gelu(x, approximate=True)

def _silu(x):
    return jax.nn.silu(x)

def _sigmoid(x):
    return jax.nn.sigmoid(x)

def _layernorm(x, axis=-1, eps=1e-05):
    m = jnp.mean(x, axis=axis, keepdims=True)
    v = jnp.var(x, axis=axis, keepdims=True)
    return (x - m) / jnp.sqrt(v + eps)

def _scatter_add(tgt, idx, src, axis=0):
    return tgt.at[idx].add(src)

def _segment_sum(src, seg, n):
    return jax.ops.segment_sum(src, seg, n)
kernel_name = 'mk_gnn_resnorm_d1_gnn_r32_58c10a'

def setup_inputs(seed: int=0):
    np.random.seed(seed)
    _w = jnp.asarray

    def _rec_inputs():
        import jax
        import jax.numpy as jnp
        _gk = jax.random.key(seed)
        x = -8.776e-05 + 1 * jax.random.normal(jax.random.fold_in(_gk, 1), (50000, 256), jnp.float32)
        src = jax.random.randint(jax.random.fold_in(_gk, 2), (25000,), 0, 50000, jnp.int32)
        dst = jnp.minimum((50000 * jax.random.uniform(jax.random.fold_in(_gk, 3), (25000,)) ** 2.0).astype(jnp.int32), 49999)
        _o = jnp.argsort(dst, stable=True)
        src = src[_o]
        dst = dst[_o]
        edge_attr_256 = 2.93046e-05 + 1.00006 * jax.random.normal(jax.random.fold_in(_gk, 11), (25000, 256), jnp.float32)
        return (x, src, dst, edge_attr_256)
    x, src, dst, edge_attr_256 = _rec_inputs()

    def _L0_gnn_setup():
        import jax, jax.numpy as jnp
        import numpy as np
        N, E, D = (625, 10000, 256)
        H, C = (8, 32)
        key = jax.random.key(seed)
        ks = jax.random.split(key, 12)
        s = 1.0 / np.sqrt(D)
        return {'x': jax.random.normal(ks[0], (N, D), jnp.float32), 'edge_index': jax.random.randint(ks[1], (2, E), 0, N, jnp.int64), 'edge_attr': jax.random.normal(ks[2], (E, D), jnp.float32), 'Wq': jax.random.normal(ks[3], (D, H * C), jnp.float32) * s, 'bq': jnp.zeros((H * C,), jnp.float32), 'Wk': jax.random.normal(ks[4], (D, H * C), jnp.float32) * s, 'bk': jnp.zeros((H * C,), jnp.float32), 'Wv': jax.random.normal(ks[5], (D, H * C), jnp.float32) * s, 'bv': jnp.zeros((H * C,), jnp.float32), 'We': jax.random.normal(ks[6], (D, H * C), jnp.float32) * s, 'Ws': jax.random.normal(ks[7], (D, H * C), jnp.float32) * s, 'bs': jnp.zeros((H * C,), jnp.float32)}
    _L0_gnn_all = _L0_gnn_setup()
    _L0_gnn_in = {k: v for k, v in _L0_gnn_all.items() if k in ('Wq', 'bq', 'Wk', 'bk', 'Wv', 'bv', 'We', 'Ws', 'bs')}
    del _L0_gnn_all
    return {'x': x, 'src': src, 'dst': dst, 'edge_attr_256': edge_attr_256, 'L0_gnn_Wq': _L0_gnn_in['Wq'], 'L0_gnn_bq': _L0_gnn_in['bq'], 'L0_gnn_Wk': _L0_gnn_in['Wk'], 'L0_gnn_bk': _L0_gnn_in['bk'], 'L0_gnn_Wv': _L0_gnn_in['Wv'], 'L0_gnn_bv': _L0_gnn_in['bv'], 'L0_gnn_We': _L0_gnn_in['We'], 'L0_gnn_Ws': _L0_gnn_in['Ws'], 'L0_gnn_bs': _L0_gnn_in['bs']}

def reference(x, src, dst, edge_attr_256, L0_gnn_Wq, L0_gnn_bq, L0_gnn_Wk, L0_gnn_bk, L0_gnn_Wv, L0_gnn_bv, L0_gnn_We, L0_gnn_Ws, L0_gnn_bs):
    import jax
    import jax.numpy as jnp

    def _L0_gnn_ref(x, edge_index, edge_attr, Wq, bq, Wk, bk, Wv, bv, We, Ws, bs):
        import jax, jax.numpy as jnp
        import numpy as np
        N, E, D = (625, 10000, 256)
        H, C = (8, 32)
        n = x.shape[0]
        src, dst = (edge_index[0], edge_index[1])
        q = (x @ Wq + bq).reshape(n, H, C)
        k = (x @ Wk + bk).reshape(n, H, C)
        v = (x @ Wv + bv).reshape(n, H, C)
        e = (edge_attr @ We).reshape(-1, H, C)
        kj = k[src] + e
        alpha = jnp.einsum('ehc,ehc->eh', q[dst], kj) / jnp.sqrt(jnp.float32(C))
        amax = jax.ops.segment_max(alpha, dst, num_segments=n)
        ea = jnp.exp(alpha - amax[dst])
        denom = jax.ops.segment_sum(ea, dst, num_segments=n)
        alpha = ea / (denom[dst] + 1e-16)
        msg = (v[src] + e) * alpha[:, :, None]
        out = jax.ops.segment_sum(msg, dst, num_segments=n)
        out = out.reshape(n, H * C) + (x @ Ws + bs)
        return out
    edge_index = jnp.stack([src, dst])
    x = _layernorm(x + _L0_gnn_ref(x, edge_index, edge_attr_256, L0_gnn_Wq, L0_gnn_bq, L0_gnn_Wk, L0_gnn_bk, L0_gnn_Wv, L0_gnn_bv, L0_gnn_We, L0_gnn_Ws, L0_gnn_bs), axis=-1)
    return x

_drawn_inputs = setup_inputs


def setup_inputs(seed=0):
    import zlib

    import numpy as np

    out = dict(_drawn_inputs(seed))
    spreads = {'L0_gnn_bq': (0.0, 0.67),
     'L0_gnn_bk': (0.0, 0.8),
     'L0_gnn_bv': (0.0, 0.1),
     'L0_gnn_bs': (0.0, 0.1)}
    factors = {}
    for name, (base, spread) in spreads.items():
        noise = np.random.default_rng([zlib.crc32(name.encode()), seed]).standard_normal(out[name].shape)
        drawn = base * np.exp(spread * noise) if base else spread * noise
        out[name] = jnp.asarray(drawn.astype(out[name].dtype))
    for name, factor in factors.items():
        out[name] = (out[name] * factor).astype(out[name].dtype)
    return out
```

```python
from contextlib import ExitStack

import numpy as np

import concourse.bass as bass
from concourse import mybir

P = 128
D = 256
KC = D // P
H = 8
C = D // H
N = 50000
E = 25000

NG = 8
EG = 4
NODE_GROUPS = -(-N // (P * NG))
EDGE_GROUPS = -(-E // (P * EG))
NP = NODE_GROUPS * P * NG
TILES = EDGE_GROUPS * EG
EP = TILES * P
ENTRIES = 2 * TILES
EB = 4
EW = ENTRIES // EB
REC = 2 * D + 2 * H
SKIP = float(1 << 20)
FAR = 1.5e38
EPS = 1e-5
TINY = 1e-16
SCALE = float(C) ** -0.5

assert EDGE_GROUPS % 2 == 1 and NODE_GROUPS % 2 == 1 and ENTRIES % EB == 0 and EW <= P

ALU = mybir.AluOpType
ACT = mybir.ActivationFunctionType
AX = mybir.AxisListType
F32 = mybir.dt.float32
BF16 = mybir.dt.bfloat16
I32 = mybir.dt.int32


def over(eng, sem, value):
    if not (isinstance(value, int) and value <= 0):
        eng.wait_ge(sem, value)


def apart(eng, passed, *waits):
    counts = [v if isinstance(v, int) else eng.lower_val(v) for _, v in waits]
    eng.wait_ge(*passed)
    for (sem, _), value in zip(waits, counts):
        over(eng, sem, value)


def wide(ap, n):
    return ap.unsqueeze(2).to_broadcast([ap.shape[0], ap.shape[1], n])


def build(nc, xt, xrows, et, slots, dst_row, flag_rows, cols, edge_ends, entry_cols, entry_row,
          wq, bq, wk, bk, wv, bv, we, ws, bs, out):
    bounds = nc.dram_tensor("bounds", [ENTRIES, REC], F32)
    with ExitStack() as ctx:
        def sb(name, shape, dt=F32):
            return ctx.enter_context(nc.sbuf_tensor(name, shape, dt))

        def sem(name):
            return ctx.enter_context(nc.semaphore(name))

        bank = [ctx.enter_context(nc.psum_tensor(f"bank{i}", [P, 512], F32)) for i in range(8)]

        ident = sb("ident", [P, P])
        ones = sb("ones", [P, P], BF16)
        half = sb("half", [P, NG])
        w_kv = sb("w_kv", [P, KC, 2 * D])
        w_qs = sb("w_qs", [P, KC, 2 * D])
        w_e = sb("w_e", [P, KC, D])
        bias = sb("bias", [P, 4 * D])
        part1 = sb("part1", [P, 4 * D], BF16)
        part2 = sb("part2", [P, 4 * D], BF16)
        part3 = sb("part3", [P, 4 * D], BF16)
        bias3 = sb("bias3", [P, 4 * D], BF16)
        mean = sb("mean", [P, KC + 1])
        flag_i = sb("flag_i", [EG * H, EDGE_GROUPS, P], I32)
        flag = sb("flag", [EG * H, EDGE_GROUPS, P + 1])
        col_i = sb("col_i", [P, 2, TILES], I32)
        end_i = sb("end_i", [P, 2, TILES], I32)
        col_f = sb("col_f", [P, TILES])
        inner = sb("inner", [P, 3, TILES])
        where = sb("where", [P, TILES], I32)

        xT = [sb(f"xT{p}", [P, KC, NG, P]) for p in range(2)]
        y = [sb(f"y{p}", [P, NG, D]) for p in range(2)]
        rest, rest2 = (a[:, 0:4, :].rearrange("p j d -> p (j d)") for a in y)
        square = [sb(f"square{i}", [P, D]) for i in range(2)]
        ssq = [sb(f"ssq{p}", [P, NG]) for p in range(2)]
        var = [sb(f"var{p}", [P, NG]) for p in range(2)]
        rstd = [sb(f"rstd{p}", [P, NG]) for p in range(2)]

        slot = [sb(f"slot{p}", [P, EG, 2], I32) for p in range(2)]
        goto = [sb(f"goto{p}", [P, EG], I32) for p in range(2)]
        eT = [sb(f"eT{h}", [P, 2, KC, P]) for h in range(2)]
        dst_all = [sb(f"dst_all{p}", [P, EG * P], I32) for p in range(2)]
        rows_in = [sb(f"rows_in{j}", [P, 2, D]) for j in range(EG)]
        sdT = [sb(f"sdT{i}", [P, 2, KC, P]) for i in range(2)]
        e_sb = [sb(f"e_sb{i}", [P, D]) for i in range(2)]
        qs = [[sb(f"qs{p}{j}", [P, 2 * D]) for j in range(EG)] for p in range(2)]
        kv = [[sb(f"kv{p}{j}", [P, 2 * D]) for j in range(EG)] for p in range(2)]
        prod = sb("prod", [P, D])
        alpha = [sb(f"alpha{p}", [P, EG * H]) for p in range(2)]
        same = [[sb(f"same{p}{j}", [P, P]) for j in range(EG)] for p in range(2)]
        at = sb("at", [EG * H, P + 1])
        run = sb("run", [EG * H, P])
        peak = sb("peak", [EG * H, P])
        below = sb("below", [P, EG * H])
        mv = sb("mv", [P, EG, D + H])
        dr = [sb(f"dr{p}", [P, EG, 2 * H]) for p in range(2)]
        den = sb("den", [P, EG * H])
        rden = sb("rden", [P, EG * H])
        avg = [sb(f"avg{p}", [P, EG, D]) for p in range(2)]
        z = [sb(f"z{p}", [P, EG, D]) for p in range(2)]
        stats = sb("stats", [P, EG, 6])
        moments = sb("moments", [P, EG, 2])
        vare = sb("vare", [P, EG])
        rstd2 = sb("rstd2", [P, EG])

        rec = sb("rec", [EW, EB, REC])
        ent_i = sb("ent_i", [EW, 3, EB], I32)
        ent_f = sb("ent_f", [EW, EB])
        erow_i = sb("erow_i", [P, ENTRIES], I32)
        eflag = sb("eflag", [H, ENTRIES + 1])
        esame = [xT[1][0:EW].rearrange("p c j n -> p (c j n)")[:, i * ENTRIES:(i + 1) * ENTRIES]
                 for i in range(EB)]
        erun, epeak = (xT[0][0:H].rearrange("p c j n -> p (c j n)")[:, i * ENTRIES:(i + 1) * ENTRIES]
                       for i in range(2))
        ebelow = sb("ebelow", [EW, EB * H])
        ep = sb("ep", [EW, EB * H])
        ekeep = sb("ekeep", [EW, EB])
        emv = y[0][0:EW].rearrange("p j d -> p (j d)")[:, 0:EB * (D + H)].rearrange("p (b w) -> p b w", b=EB)
        egoto = sb("egoto", [EW, EB], I32)
        enext = sb("enext", [EW, EB])
        eden = sb("eden", [EW, EB * H])
        erden = sb("erden", [EW, EB * H])
        ez = y[1][0:EW, 0:EB, :]
        estats = sb("estats", [EW, EB, 6])
        emoments = sb("emoments", [EW, EB, 2])
        evar = sb("evar", [EW, EB])
        erstd = sb("erstd", [EW, EB])

        loaded_w = sem("loaded_w")
        loaded_i = sem("loaded_i")
        pool_const = sem("pool_const")
        step = sem("step")
        consts = sem("consts")
        x_in = [sem(f"x_in{p}") for p in range(2)]
        node_mm = sem("node_mm")
        biased = sem("biased")
        squared = sem("squared")
        var_ready = sem("var_ready")
        rstd_ready = sem("rstd_ready")
        node_rows = sem("node_rows")
        stored = [sem(f"stored{p}") for p in range(2)]

        slots_in = [sem(f"slots_in{p}") for p in range(2)]
        dst_in = [sem(f"dst_in{p}") for p in range(2)]
        e_in = [sem(f"e_in{h}") for h in range(2)]
        gathered = [sem(f"gathered{j}") for j in range(EG)]
        turned = sem("turned")
        turned_sb = sem("turned_sb")
        e_mm = sem("e_mm")
        kv_mm = sem("kv_mm")
        qs_mm = sem("qs_mm")
        e_copied = sem("e_copied")
        qs_copied = sem("qs_copied")
        kv_ready = sem("kv_ready")
        prod_ready = sem("prod_ready")
        alpha_ready = sem("alpha_ready")
        same_ready = sem("same_ready")
        alpha_turned = sem("alpha_turned")
        flag_ready = sem("flag_ready")
        run_ready = sem("run_ready")
        peak_ready = sem("peak_ready")
        peak_turned = sem("peak_turned")
        below_ready = sem("below_ready")
        peak_kept = sem("peak_kept")
        p_ready = sem("p_ready")
        mv_ready = sem("mv_ready")
        summed = sem("summed")
        den_ready = sem("den_ready")
        den_kept = sem("den_kept")
        rden_ready = sem("rden_ready")
        avg_ready = sem("avg_ready")
        z_ready = sem("z_ready")
        stats_ready = sem("stats_ready")
        moments_ready = sem("moments_ready")
        vare_ready = sem("vare_ready")
        rstd2_ready = sem("rstd2_ready")
        goto_ready = sem("goto_ready")
        edge_rows = sem("edge_rows")
        scattered = [sem(f"scattered{p}") for p in range(2)]
        bound_out = [sem(f"bound_out{p}") for p in range(2)]

        rec_in = sem("rec_in")
        t_turned = sem("t_turned")
        t_step = sem("t_step")
        t_p = sem("t_p")
        t_mv = sem("t_mv")
        t_summed = sem("t_summed")
        t_var = sem("t_var")
        t_rstd = sem("t_rstd")
        t_rows = sem("t_rows")
        t_out = sem("t_out")

        turn_b, kv_b, qs_b, e_b, sum_b, small_b = bank[0], bank[1:3], bank[3], bank[4], bank[5:7], bank[7]
        aT_ps = small_b[0:EG * H, 0:P]
        peak_ps = small_b[:, P:P + EG * H]
        den_ps = small_b[:, P + EG * H:P + 2 * EG * H]

        out_groups = out.rearrange("(g p j) d -> g p j d", p=P, j=NG)
        bound_rows = bounds.ap().rearrange("(t r) w -> r t w", r=2)
        NODE_PAIRS = NG // 2
        W_LOADS, I_LOADS = 11, 1 + 1 + 2 + 1 + 1
        GO_LAST = EDGE_GROUPS - 1

        def groups(eng, body, last):
            for g in range(4):
                body(g, g % 2, g // 2)
            with eng.Fori(0, (last - 4) // 2) as m:
                body(m * 2 + 4, 0, m + 2)
                body(m * 2 + 5, 1, m + 2)
            body(last, 0, last // 2)

        def node_groups(eng, body):
            groups(eng, body, NODE_GROUPS - 1)

        def edge_groups(eng, body):
            groups(eng, body, GO_LAST)

        def is_first(g):
            return isinstance(g, int) and g == 0

        def is_early(g):
            return isinstance(g, int) and g < 2

        def is_last(g):
            return isinstance(g, int) and g == GO_LAST

        block = ctx.enter_context(nc.Block())

        @block.sync
        def _(sp):
            for src, dst in ((wk, w_kv[:, :, 0:D]), (wv, w_kv[:, :, D:]), (wq, w_qs[:, :, 0:D]),
                             (ws, w_qs[:, :, D:]), (we, w_e[:])):
                sp.dma_start(dst, src.rearrange("(c k) n -> k c n", k=P)).then_inc(loaded_w, 16)
            for i, b in enumerate((bk, bv, bq, bs)):
                sp.dma_start(bias[:, i * D:(i + 1) * D], b.partition_broadcast(P)).then_inc(loaded_w, 16)
            sp.dma_start(col_i[:], cols).then_inc(loaded_i, 16)
            for i in range(2):
                sp.dma_start(end_i[:, i, :], edge_ends[i].partition_broadcast(P)).then_inc(loaded_w, 16)
            for j in range(EG):
                sp.dma_start(flag_i[j * H:(j + 1) * H, :, :].rearrange("h g e -> h (g e)"),
                             flag_rows[j].partition_broadcast(H)).then_inc(loaded_i, 16)
            sp.dma_start(ent_i[:], entry_cols).then_inc(loaded_i, 16)
            sp.dma_start(erow_i[:], entry_row.partition_broadcast(P)).then_inc(loaded_i, 16)

            def load_x(g, par, u):
                over(sp, node_mm, (g - 1) * NODE_PAIRS)
                sp.dma_start(xT[par][:], xt[g]).then_inc(x_in[par], 16)

            node_groups(sp, load_x)

            def load_edges(g, par, u):
                over(sp, turned, (g - 1) * EG)
                sp.dma_start(slot[par][:], slots[g]).then_inc(slots_in[par], 16)
                over(sp, same_ready, (g - 1) * EG)
                sp.dma_start(dst_all[par][:], dst_row[g].partition_broadcast(P)).then_inc(dst_in[par], 16)
                for h in range(2):
                    over(sp, e_mm, (g - 1) * EG + 2 * h + 2)
                    sp.dma_start(eT[h][:], et[g * 2 + h]).then_inc(e_in[h], 16)

            def keep_bounds(g, par, u):
                sp.wait_ge(avg_ready, g * 2 + 2)
                sp.wait_ge(peak_kept, g + 1)
                sp.wait_ge(den_kept, g + 1)
                ends = slice(0, P, P - 1)
                table = bound_rows[:, bass.ds(g * EG, EG), :]
                sp.dma_start(table[:, :, 0:D], avg[par][ends, :, :]).then_inc(bound_out[par], 16)
                sp.dma_start(table[:, :, 2 * D:], dr[par][ends, :, :]).then_inc(bound_out[par], 16)
                for j in range(EG):
                    sp.dma_start(table[:, j, D:2 * D], qs[par][j][ends, D:]).then_inc(bound_out[par], 16)

            def edge_body(g, par, u):
                load_edges(g, par, u)
                if not is_early(g):
                    keep_bounds(g - 2, par, u - 1)

            edge_groups(sp, edge_body)
            keep_bounds(GO_LAST - 1, 1, 0)
            keep_bounds(GO_LAST, 0, 0)
            sp.wait_ge(bound_out[0], 16 * 6 * (GO_LAST // 2 + 1))
            sp.wait_ge(bound_out[1], 16 * 6 * (GO_LAST // 2))
            sp.dma_start(rec[:], bounds.ap().rearrange("(b i) w -> i b w", b=EB)).then_inc(rec_in, 16)
            sp.wait_ge(stored[0], 16 * (NODE_GROUPS // 2 + 1))
            sp.wait_ge(stored[1], 16 * (NODE_GROUPS // 2))
            sp.wait_ge(scattered[0], 16 * EG * (GO_LAST // 2 + 1))
            sp.wait_ge(scattered[1], 16 * EG * (GO_LAST // 2))
            sp.wait_ge(t_out, 16 * EB)

        @block.gpsimd
        def _(pool):
            nc.gpsimd.memset(ident[:], 0.0).then_inc(pool_const, 1)
            pool.wait_ge(pool_const, 1)
            nc.gpsimd.affine_select(out=ident[:], in_=ident[:], compare_op=ALU.not_equal, fill=1.0, base=0,
                                    pattern=[[-1, P]], channel_multiplier=1).then_inc(pool_const, 1)
            nc.gpsimd.memset(ones[:], 1.0).then_inc(pool_const, 1)
            nc.gpsimd.memset(half[:], -0.5).then_inc(pool_const, 1)
            pool.wait_ge(pool_const, 4)

            def nodes(g, par, u):
                pool.wait_ge(var_ready, g + 1)
                nc.gpsimd.tensor_tensor(rstd[par][:], var[par][:], half[:], ALU.pow).then_inc(rstd_ready, 1)
                pool.wait_ge(node_rows, g + 1)
                pool.dma_start(out_groups[g], y[par][:]).then_inc(stored[par], 16)

            node_groups(pool, nodes)
            pool.wait_ge(stored[0], 16 * (NODE_GROUPS // 2 + 1))
            pool.wait_ge(stored[1], 16 * (NODE_GROUPS // 2))

            def gather(g, par, u, j):
                apart(pool, (pool_const, 4), (turned, (g - 1) * EG + j + 1),
                      *[(slots_in[par], (u + 1) * 16)] * (j == 0))
                for i in range(2):
                    nc.gpsimd.indirect_dma_start(
                        out=rows_in[j][:, i, :], out_offset=None, in_=xrows,
                        in_offset=bass.IndirectOffsetOnAxis(ap=slot[par][:, j, i:i + 1], axis=0),
                    ).then_inc(gathered[j], 16)

            def add_y(g, par, u, b):
                pool.wait_ge(avg_ready, g * 2 + b + 1)
                if b == 0:
                    over(pool, scattered[par], u * 16 * EG)
                for j in (2 * b, 2 * b + 1):
                    ins = nc.gpsimd.tensor_tensor(z[par][:, j, :], avg[par][:, j, :], qs[par][j][:, D:], ALU.add)
                ins.then_inc(z_ready, 1)

            def root(g):
                pool.wait_ge(vare_ready, g + 1)
                nc.gpsimd.tensor_tensor(rstd2[:], vare[:], half[:, 0:EG], ALU.pow).then_inc(rstd2_ready, 1)

            def scatter(g, par, u):
                apart(pool, (pool_const, 4), (edge_rows, g + 1), (goto_ready, g + 1))
                for j in range(EG):
                    nc.gpsimd.indirect_dma_start(
                        out=out, out_offset=bass.IndirectOffsetOnAxis(ap=goto[par][:, j:j + 1], axis=0),
                        in_=z[par][:, j, :], in_offset=None, bounds_check=NP - 1, oob_is_err=False,
                    ).then_inc(scattered[par], 16)

            def finish(g, par, u, more):
                add_y(g, par, u, 0)
                add_y(g, par, u, 1)
                more(2)
                root(g)
                more(3)
                scatter(g, par, u)

            for j in range(EG):
                gather(0, 0, 0, j)

            def edge_body(g, par, u):
                def more(j):
                    if not is_last(g):
                        gather(g + 1, 1 - par, u + par, j)
                more(0)
                more(1)
                if is_early(g):
                    more(2)
                    more(3)
                else:
                    finish(g - 2, par, u - 1, more)

            edge_groups(pool, edge_body)
            finish(GO_LAST - 1, 1, GO_LAST // 2 - 1, lambda j: None)
            finish(GO_LAST, 0, GO_LAST // 2, lambda j: None)

            pool.wait_ge(t_var, 1)
            nc.gpsimd.tensor_tensor(erstd[:], evar[:], half[0:EW, 0:EB], ALU.pow).then_inc(t_rstd, 1)
            pool.wait_ge(t_rows, 1)
            for b in range(EB):
                nc.gpsimd.indirect_dma_start(
                    out=out, out_offset=bass.IndirectOffsetOnAxis(ap=egoto[:, b:b + 1], axis=0),
                    in_=ez[:, b, :], in_offset=None, bounds_check=NP - 1, oob_is_err=False,
                ).then_inc(t_out, 16)

        @block.scalar
        def _(act):
            def nodes(g, par, u):
                over(act, var_ready, g - 1)
                for b in range(NODE_PAIRS):
                    act.wait_ge(biased, g * NODE_PAIRS + b + 1)
                    for j in (2 * b, 2 * b + 1):
                        over(act, squared, g * NG + j - 1)
                        nc.scalar.activation(square[j % 2][:], y[par][:, j, :], ACT.Square,
                                             accum_out=ssq[par][:, j:j + 1]).then_inc(squared, 1)

            node_groups(act, nodes)

            def copy_turned(g, j):
                t = g * EG + j
                act.wait_ge(turned, t + 1)
                over(act, qs_mm, t - 1)
                nc.scalar.copy(sdT[j % 2][:].rearrange("p a c e -> p (a c e)"), turn_b[:]).then_inc(turned_sb, 1)

            def tile(g, par, u, j):
                t = g * EG + j
                if not (is_last(g) and j == EG - 1):
                    copy_turned(g, j + 1) if j < EG - 1 else copy_turned(g + 1, 0)
                act.wait_ge(e_mm, t + 1)
                over(act, kv_ready, t - 1)
                nc.scalar.copy(e_sb[j % 2][:], e_b[:, 0:D]).then_inc(e_copied, 1)
                if j == 2 and not is_first(g):
                    weigh(g - 1)
                act.wait_ge(qs_mm, t + 1)
                if j == 0:
                    over(act, z_ready, (g - 1) * 2)
                    if not is_early(g):
                        act.wait_ge(bound_out[par], u * 16 * 6)
                nc.scalar.copy(qs[par][j][:], qs_b[:]).then_inc(qs_copied, 1)

            def weigh(g):
                act.wait_ge(below_ready, g + 1)
                over(act, summed, g)
                nc.scalar.activation(mv[:, :, D:], below[:].rearrange("p (j h) -> p j h", h=H), ACT.Exp,
                                     scale=SCALE).then_inc(p_ready, 1)

            act.wait_ge(squared, NODE_GROUPS * NG)
            copy_turned(0, 0)

            def edge_body(g, par, u):
                for j in range(EG):
                    tile(g, par, u, j)

            edge_groups(act, edge_body)
            weigh(GO_LAST)
            act.wait_ge(t_step, 4)
            nc.scalar.activation(ep[:], ebelow[:], ACT.Exp, scale=SCALE).then_inc(t_p, 1)

        @block.vector
        def _(dve):
            made = [0]

            def then(ins):
                made[0] += 1
                ins.then_inc(step, 1)
                dve.wait_ge(step, made[0])

            dve.wait_ge(loaded_w, 16 * W_LOADS)
            dve.wait_ge(pool_const, 4)
            for c in range(KC):
                diag = w_qs[:, c, D + c * P:D + (c + 1) * P]
                then(nc.vector.tensor_tensor(diag, diag, ident[:], ALU.add))
            then(nc.vector.tensor_reduce(mean[:, 0:KC], w_qs[:, :, D:], AX.X, ALU.add))
            then(nc.vector.tensor_reduce(mean[:, KC:], bias[:, 3 * D:], AX.X, ALU.add))
            then(nc.vector.tensor_scalar(mean[:], mean[:], 1.0 / D, None, ALU.mult))
            for c in range(KC):
                w = w_qs[:, c, D:]
                nc.vector.tensor_scalar(w, w, mean[:, c:c + 1], None, ALU.subtract)
            then(nc.vector.tensor_scalar(bias[:, 3 * D:], bias[:, 3 * D:], mean[:, KC:], None, ALU.subtract))
            then(nc.vector.tensor_copy(part1[:], bias[:]))
            then(nc.vector.tensor_tensor(rest, bias[:], part1[:], ALU.subtract))
            then(nc.vector.tensor_copy(part2[:], rest))
            then(nc.vector.tensor_tensor(rest2, rest, part2[:], ALU.subtract))
            then(nc.vector.tensor_copy(part3[:], rest2))
            then(nc.vector.tensor_scalar(part1[:], part1[:], ident[:, 0:1], None, ALU.mult))
            then(nc.vector.scalar_tensor_tensor(out=part2[:], in0=part2[:], scalar=ident[:, 1:2], in1=part1[:],
                                                op0=ALU.mult, op1=ALU.add))
            then(nc.vector.scalar_tensor_tensor(out=bias3[:], in0=part3[:], scalar=ident[:, 2:3], in1=part2[:],
                                                op0=ALU.mult, op1=ALU.add))
            nc.vector.engine_nop().then_inc(consts, 1)

            def nodes(g, par, u):
                over(dve, stored[par], u * 16)
                for b in range(NODE_PAIRS):
                    dve.wait_ge(node_mm, g * NODE_PAIRS + b + 1)
                    nc.vector.tensor_tensor(
                        y[par][:, 2 * b:2 * b + 2, :],
                        bank[par * NODE_PAIRS + b][:].rearrange("p (j d) -> p j d", j=2),
                        bias[:, 3 * D:].unsqueeze(1).to_broadcast([P, 2, D]), ALU.add).then_inc(biased, 1)
                dve.wait_ge(squared, (g + 1) * NG)
                over(dve, rstd_ready, g - 1)
                nc.vector.tensor_scalar(var[par][:], ssq[par][:], 1.0 / D, EPS, ALU.mult, ALU.add).then_inc(var_ready, 1)
                dve.wait_ge(rstd_ready, g + 1)
                for j in range(NG):
                    ins = nc.vector.tensor_scalar(y[par][:, j, :], y[par][:, j, :], rstd[par][:, j:j + 1],
                                                  None, ALU.mult)
                ins.then_inc(node_rows, 1)

            node_groups(dve, nodes)

            dve.wait_ge(loaded_i, 16 * (1 + EG + 2))
            nc.vector.memset(flag[:, :, 0:1], -FAR)
            nc.vector.memset(flag[:, :, P:P + 1], -FAR)
            then(nc.vector.tensor_tensor(flag[:, :, 1:P], flag_i[:, :, 1:P], flag_i[:, :, 0:P - 1], ALU.not_equal))
            then(nc.vector.tensor_scalar(flag[:, :, 1:P], flag[:, :, 1:P], -FAR, None, ALU.mult))
            then(nc.vector.tensor_copy(col_f[:], col_i[:, 0, :]))
            then(nc.vector.tensor_tensor(inner[:, 0, :], col_i[:, 0, :], col_i[:, 1, :], ALU.is_equal))
            then(nc.vector.tensor_tensor(inner[:, 1, :], col_i[:, 0, :], end_i[:, 0, :], ALU.is_equal))
            then(nc.vector.tensor_tensor(inner[:, 2, :], col_i[:, 0, :], end_i[:, 1, :], ALU.is_equal))
            then(nc.vector.tensor_tensor(inner[:, 0, :], inner[:, 0, :], inner[:, 1, :], ALU.max))
            then(nc.vector.tensor_tensor(inner[:, 0, :], inner[:, 0, :], inner[:, 2, :], ALU.max))
            then(nc.vector.scalar_tensor_tensor(out=where[:], in0=inner[:, 0, :], scalar=SKIP, in1=col_f[:],
                                                op0=ALU.mult, op1=ALU.add))

            def tile(g, par, u, j):
                t = g * EG + j
                dve.wait_ge(kv_mm, t + 1)
                dve.wait_ge(e_copied, t + 1)
                if j == 0:
                    over(dve, mv_ready, g - 1)
                nc.vector.tensor_tensor(kv[par][j][:].rearrange("p (a d) -> p a d", a=2),
                                        kv_b[j % 2][:].rearrange("p (a d) -> p a d", a=2),
                                        e_sb[j % 2][:].unsqueeze(1).to_broadcast([P, 2, D]),
                                        ALU.add).then_inc(kv_ready, 1)
                if j == 0:
                    dve.wait_ge(dst_in[par], (u + 1) * 16)
                    over(dve, summed, g - 1)
                nc.vector.tensor_scalar(same[par][j][:], dst_all[par][:, j * P:(j + 1) * P],
                                        col_f[:, bass.ds(t, 1)], None, ALU.is_equal).then_inc(same_ready, 1)
                dve.wait_ge(qs_copied, t + 1)
                dve.wait_ge(kv_ready, t + 1)
                over(dve, alpha_ready, t)
                nc.vector.tensor_tensor(prod[:], kv[par][j][:, 0:D], qs[par][j][:, 0:D],
                                        ALU.mult).then_inc(prod_ready, 1)
                dve.wait_ge(prod_ready, t + 1)
                if j == 0:
                    over(dve, alpha_turned, g - 1)
                    over(dve, below_ready, g - 1)
                nc.vector.tensor_reduce(alpha[par][:, j * H:(j + 1) * H],
                                        prod[:].rearrange("p (h c) -> p h c", h=H), AX.X,
                                        ALU.add).then_inc(alpha_ready, 1)

            def maxima(g):
                over(dve, peak_ready, g)
                nc.vector.tensor_copy(at[:], flag[:, bass.ds(g, 1), :].rearrange("p o e -> p (o e)")).then_inc(flag_ready, 1)
                dve.wait_ge(flag_ready, g + 1)
                dve.wait_ge(alpha_turned, g + 1)
                nc.vector.tensor_tensor_scan(run[:], at[:, 0:P], aT_ps, -FAR, ALU.add, ALU.max).then_inc(run_ready, 1)
                dve.wait_ge(run_ready, g + 1)
                over(dve, peak_turned, g)
                nc.vector.tensor_tensor_scan(peak[:, ::-1], at[:, 1:P + 1][:, ::-1], run[:, ::-1], -FAR,
                                             ALU.add, ALU.max).then_inc(peak_ready, 1)

            def shift(g, par, u):
                dve.wait_ge(peak_turned, g + 1)
                over(dve, p_ready, g)
                nc.vector.tensor_tensor(below[:], alpha[par][:], peak_ps, ALU.subtract).then_inc(below_ready, 1)
                over(dve, bound_out[par], u * 16 * 6)
                nc.vector.tensor_copy(dr[par][:, :, H:], peak_ps.rearrange("p (j h) -> p j h", h=H)).then_inc(peak_kept, 1)

            def weigh(g, par):
                dve.wait_ge(p_ready, g + 1)
                over(dve, summed, g)
                for j in range(EG):
                    ins = nc.vector.tensor_tensor(
                        mv[:, j, 0:D].rearrange("p (h c) -> p h c", h=H),
                        kv[par][j][:, D:].rearrange("p (h c) -> p h c", h=H),
                        wide(mv[:, j, D:], C), ALU.mult)
                ins.then_inc(mv_ready, 1)

            def average(g, par, u):
                dve.wait_ge(summed, g + 1)
                over(dve, rden_ready, g)
                nc.vector.tensor_scalar(den[:], den_ps, TINY, None, ALU.add).then_inc(den_ready, 1)
                nc.vector.tensor_copy(dr[par][:, :, 0:H], den_ps.rearrange("p (j h) -> p j h", h=H)).then_inc(den_kept, 1)
                dve.wait_ge(den_ready, g + 1)
                over(dve, avg_ready, g * 2)
                nc.vector.reciprocal(rden[:], den[:]).then_inc(rden_ready, 1)
                dve.wait_ge(rden_ready, g + 1)
                over(dve, bound_out[par], u * 16 * 6)
                for b in range(2):
                    nc.vector.tensor_tensor(
                        avg[par][:, 2 * b:2 * b + 2, :].rearrange("p j (h c) -> p (j h) c", h=H),
                        sum_b[b][:].rearrange("p (h c) -> p h c", c=C),
                        wide(rden[:, 2 * b * H:(2 * b + 2) * H], C), ALU.mult).then_inc(avg_ready, 1)

            def spread(g, par):
                dve.wait_ge(z_ready, g * 2 + 2)
                over(dve, moments_ready, g)
                for j in range(EG):
                    ins = nc.vector.bn_stats(stats[:, j, :], z[par][:, j, :])
                ins.then_inc(stats_ready, 1)
                apart(dve, (pool_const, 4), (stats_ready, g + 1), (edge_rows, g))
                for j in range(EG):
                    ins = nc.vector.bn_aggr(moments[:, j, :], stats[:, j, :])
                ins.then_inc(moments_ready, 1)
                dve.wait_ge(moments_ready, g + 1)
                over(dve, rstd2_ready, g)
                nc.vector.tensor_scalar(vare[:], moments[:, :, 1], EPS, None, ALU.add).then_inc(vare_ready, 1)

            def rows(g, par, u):
                over(dve, scattered[par], u * 16 * EG)
                nc.vector.tensor_copy(goto[par][:], where[:, bass.ds(g * EG, EG)]).then_inc(goto_ready, 1)
                dve.wait_ge(rstd2_ready, g + 1)
                for j in range(EG):
                    ins = nc.vector.tensor_scalar(z[par][:, j, :], z[par][:, j, :], moments[:, j, 0:1],
                                                  rstd2[:, j:j + 1], ALU.subtract, ALU.mult)
                ins.then_inc(edge_rows, 1)

            def edge_body(g, par, u):
                if not is_early(g):
                    average(g - 2, par, u - 1)
                tile(g, par, u, 0)
                if not is_first(g):
                    maxima(g - 1)
                tile(g, par, u, 1)
                if not is_first(g):
                    shift(g - 1, 1 - par, u - 1 + par)
                if not is_early(g):
                    spread(g - 2, par)
                tile(g, par, u, 2)
                if not is_first(g):
                    weigh(g - 1, 1 - par)
                if not is_early(g):
                    rows(g - 2, par, u - 1)
                tile(g, par, u, 3)

            edge_groups(dve, edge_body)
            last_u = GO_LAST // 2
            average(GO_LAST - 1, 1, last_u - 1)
            maxima(GO_LAST)
            shift(GO_LAST, 0, last_u)
            weigh(GO_LAST, 0)
            spread(GO_LAST - 1, 1)
            rows(GO_LAST - 1, 1, last_u - 1)
            average(GO_LAST, 0, last_u)
            spread(GO_LAST, 0)
            rows(GO_LAST, 0, last_u)

            t_made = [0]

            def t_then(ins):
                t_made[0] += 1
                ins.then_inc(t_step, 1)
                dve.wait_ge(t_step, t_made[0])

            nc.vector.memset(eflag[:, 0:1], -FAR)
            nc.vector.memset(eflag[:, ENTRIES:], -FAR)
            then(nc.vector.tensor_tensor(eflag[:, 1:ENTRIES], erow_i[0:H, 1:], erow_i[0:H, 0:ENTRIES - 1], ALU.not_equal))
            then(nc.vector.tensor_scalar(eflag[:, 1:ENTRIES], eflag[:, 1:ENTRIES], -FAR, None, ALU.mult))
            then(nc.vector.tensor_copy(ent_f[:], ent_i[:, 0, :]))
            then(nc.vector.tensor_tensor(ekeep[:], ent_i[:, 0, :], ent_i[:, 1, :], ALU.not_equal))
            then(nc.vector.tensor_tensor(enext[:], ent_i[:, 0, :], ent_i[:, 2, :], ALU.is_equal))
            then(nc.vector.scalar_tensor_tensor(out=egoto[:], in0=enext[:], scalar=SKIP, in1=ent_f[:],
                                                op0=ALU.mult, op1=ALU.add))
            for i in range(EB):
                ins = nc.vector.tensor_scalar(esame[i], erow_i[0:EW, :], ent_f[:, i:i + 1], None, ALU.is_equal)
            then(ins)
            dve.wait_ge(t_turned, 1)
            t_then(nc.vector.tensor_tensor_scan(erun, eflag[:, 0:ENTRIES], kv_b[0][0:H, 0:ENTRIES], -FAR,
                                                ALU.add, ALU.max))
            t_then(nc.vector.tensor_tensor_scan(epeak[:, ::-1], eflag[:, 1:][:, ::-1], erun[:, ::-1], -FAR,
                                                ALU.add, ALU.max))
            dve.wait_ge(t_turned, 2)
            dve.wait_ge(rec_in, 16)
            t_then(nc.vector.tensor_tensor(ebelow[:].rearrange("p (b h) -> p b h", h=H), rec[:, :, 2 * D + H:],
                                           kv_b[1][0:EW, 0:EB * H].rearrange("p (b h) -> p b h", h=H), ALU.subtract))
            t_then(nc.vector.tensor_tensor(emv[:, :, D:], rec[:, :, 2 * D:2 * D + H], wide(ekeep[:], H), ALU.mult))
            dve.wait_ge(t_p, 1)
            t_then(nc.vector.tensor_tensor(emv[:, :, D:], emv[:, :, D:], ep[:].rearrange("p (b h) -> p b h", h=H), ALU.mult))
            for b in range(EB):
                ins = nc.vector.tensor_tensor(emv[:, b, 0:D].rearrange("p (h c) -> p h c", h=H),
                                              rec[:, b, 0:D].rearrange("p (h c) -> p h c", h=H),
                                              wide(emv[:, b, D:], C), ALU.mult)
            ins.then_inc(t_mv, 1)
            for b in range(EB):
                dve.wait_ge(t_summed, b + 1)
                t_then(nc.vector.tensor_scalar(eden[:, b * H:(b + 1) * H], bank[3 + b][0:EW, D:D + H], TINY, None, ALU.add))
                t_then(nc.vector.reciprocal(erden[:, b * H:(b + 1) * H], eden[:, b * H:(b + 1) * H]))
                t_then(nc.vector.tensor_tensor(ez[:, b, :].rearrange("p (h c) -> p h c", h=H),
                                               bank[3 + b][0:EW, 0:D].rearrange("p (h c) -> p h c", h=H),
                                               wide(erden[:, b * H:(b + 1) * H], C), ALU.mult))
                t_then(nc.vector.tensor_tensor(ez[:, b, :], ez[:, b, :], rec[:, b, D:2 * D], ALU.add))
                t_then(nc.vector.bn_stats(estats[:, b, :], ez[:, b, :]))
                t_then(nc.vector.bn_aggr(emoments[:, b, :], estats[:, b, :]))
            nc.vector.tensor_scalar(evar[:], emoments[:, :, 1], EPS, None, ALU.add).then_inc(t_var, 1)
            dve.wait_ge(t_rstd, 1)
            for b in range(EB):
                ins = nc.vector.tensor_scalar(ez[:, b, :], ez[:, b, :], emoments[:, b, 0:1], erstd[:, b:b + 1],
                                              ALU.subtract, ALU.mult)
            ins.then_inc(t_rows, 1)

        @block.tensor
        def _(pe):
            pe.wait_ge(consts, 1)

            def nodes(g, par, u):
                pe.wait_ge(x_in[par], (u + 1) * 16)
                for b in range(NODE_PAIRS):
                    over(pe, biased, (g - 2) * NODE_PAIRS + b + 1)
                    for i in range(2):
                        for c in range(KC):
                            ins = nc.tensor.matmul(bank[par * NODE_PAIRS + b][:, i * D:(i + 1) * D],
                                                   xT[par][:, c, 2 * b + i, :], w_qs[:, c, D:],
                                                   start=(c == 0), stop=(c == KC - 1))
                    ins.then_inc(node_mm, 1)

            node_groups(pe, nodes)
            pe.wait_ge(biased, NODE_GROUPS * NODE_PAIRS)

            def turn(g, j):
                t = g * EG + j
                pe.wait_ge(gathered[j], (g + 1) * 32)
                over(pe, turned_sb, t)
                for i in range(2):
                    for c in range(KC):
                        ins = nc.tensor.transpose(turn_b[:, (i * KC + c) * P:(i * KC + c + 1) * P],
                                                  rows_in[j][:, i, c * P:(c + 1) * P], ident[:])
                ins.then_inc(turned, 1)

            def tile(g, par, u, j):
                t = g * EG + j
                if not (is_last(g) and j == EG - 1):
                    turn(g, j + 1) if j < EG - 1 else turn(g + 1, 0)
                if j % 2 == 0:
                    pe.wait_ge(e_in[j // 2], (g + 1) * 16)
                over(pe, e_copied, t)
                for c in range(KC):
                    ins = nc.tensor.matmul(e_b[:, 0:D], eT[j // 2][:, j % 2, c, :], w_e[:, c, :],
                                           start=(c == 0), stop=(c == KC - 1))
                ins.then_inc(e_mm, 1)
                pe.wait_ge(turned_sb, t + 1)
                over(pe, kv_ready, t - 1)
                nc.tensor.matmul(kv_b[j % 2][:], ones[:], bias3[:, 0:2 * D], start=True, stop=False)
                for c in range(KC):
                    ins = nc.tensor.matmul(kv_b[j % 2][:], sdT[j % 2][:, 0, c, :], w_kv[:, c, :],
                                           start=False, stop=(c == KC - 1))
                ins.then_inc(kv_mm, 1)
                over(pe, qs_copied, t)
                nc.tensor.matmul(qs_b[:], ones[:], bias3[:, 2 * D:], start=True, stop=False)
                for c in range(KC):
                    ins = nc.tensor.matmul(qs_b[:], sdT[j % 2][:, 1, c, :], w_qs[:, c, :],
                                           start=False, stop=(c == KC - 1))
                ins.then_inc(qs_mm, 1)

            def turn_alpha(g, par):
                pe.wait_ge(alpha_ready, (g + 1) * EG)
                over(pe, den_kept, g)
                nc.tensor.transpose(aT_ps, alpha[par][:], ident[:]).then_inc(alpha_turned, 1)

            def turn_peak(g):
                apart(pe, (consts, 1), (peak_ready, g + 1))
                nc.tensor.transpose(peak_ps, peak[:], ident[0:EG * H, 0:EG * H]).then_inc(peak_turned, 1)

            def add_up(g, par):
                pe.wait_ge(mv_ready, g + 1)
                pe.wait_ge(peak_kept, g + 1)
                pe.wait_ge(same_ready, (g + 1) * EG)
                over(pe, avg_ready, g * 2)
                for j in range(EG):
                    nc.tensor.matmul(sum_b[j // 2][:, (j % 2) * D:(j % 2 + 1) * D], same[par][j][:],
                                     mv[:, j, 0:D], start=True, stop=True)
                    ins = nc.tensor.matmul(den_ps[:, j * H:(j + 1) * H], same[par][j][:], mv[:, j, D:],
                                           start=True, stop=True)
                ins.then_inc(summed, 1)

            turn(0, 0)

            def edge_body(g, par, u):
                tile(g, par, u, 0)
                if not is_first(g):
                    turn_alpha(g - 1, 1 - par)
                tile(g, par, u, 1)
                if not is_first(g):
                    turn_peak(g - 1)
                tile(g, par, u, 2)
                tile(g, par, u, 3)
                if not is_first(g):
                    add_up(g - 1, 1 - par)

            edge_groups(pe, edge_body)
            turn_alpha(GO_LAST, 0)
            turn_peak(GO_LAST)
            add_up(GO_LAST, 0)

            pe.wait_ge(rec_in, 16)
            for b in range(EB):
                ins = nc.tensor.transpose(kv_b[0][0:H, b * EW:(b + 1) * EW], rec[:, b, 2 * D + H:],
                                          ident[0:EW, 0:EW])
            ins.then_inc(t_turned, 1)
            pe.wait_ge(t_step, 2)
            for b in range(EB):
                ins = nc.tensor.transpose(kv_b[1][0:EW, b * H:(b + 1) * H], epeak[:, b * EW:(b + 1) * EW],
                                          ident[0:H, 0:H])
            ins.then_inc(t_turned, 1)
            pe.wait_ge(t_mv, 1)
            pe.wait_ge(avg_ready, 2 * EDGE_GROUPS)
            for b in range(EB):
                for i in range(EB):
                    ins = nc.tensor.matmul(bank[3 + b][0:EW, 0:D + H], esame[i][:, b * EW:(b + 1) * EW],
                                           emv[:, i, :], start=(i == 0), stop=(i == EB - 1))
                ins.then_inc(t_summed, 1)

    return nc


def kernel(x, src, dst, edge_attr_256, L0_gnn_Wq, L0_gnn_bq, L0_gnn_Wk, L0_gnn_bk, L0_gnn_Wv, L0_gnn_bv,
           L0_gnn_We, L0_gnn_Ws, L0_gnn_bs):
    import concourse.bacc as bacc
    from concourse.bass_utils import run_bass_kernel_spmd

    x, src, dst, ea = (np.asarray(a) for a in (x, src, dst, edge_attr_256))
    xp = np.zeros((NP, D), x.dtype)
    xp[:N] = x
    ep = np.zeros((EP, D), ea.dtype)
    ep[:E] = ea
    sp = np.zeros(EP, src.dtype)
    sp[:E] = src
    dp = np.full(EP, N, dst.dtype)
    dp[:E] = dst

    tiles = dp.reshape(TILES, P)
    nxt = np.concatenate([dp[1:], dp[-1:]]).reshape(TILES, P)
    entry = tiles[:, [0, P - 1]]
    other = np.stack([np.full(TILES, -1, dst.dtype), tiles[:, 0]], 1)
    entry_next = np.concatenate([entry.ravel()[1:], np.full(1, -1, dst.dtype)])

    def by_block(a):
        return a.reshape(EB, EW).T

    arrays = {
        "xt": xp.reshape(NODE_GROUPS, P, NG, KC, P).transpose(0, 4, 3, 2, 1),
        "xrows": xp,
        "et": ep.reshape(EDGE_GROUPS * 2, 2, P, KC, P).transpose(0, 4, 1, 3, 2),
        "slots": np.stack([sp, dp], 1).reshape(EDGE_GROUPS, EG, P, 2).transpose(0, 2, 1, 3),
        "dst_row": dp.reshape(EDGE_GROUPS, EG * P),
        "flag_rows": dp.reshape(EDGE_GROUPS, EG, P).transpose(1, 0, 2).reshape(EG, EDGE_GROUPS * P),
        "cols": np.stack([tiles.T, nxt.T], 1),
        "edge_ends": entry.T,
        "entry_cols": np.stack([by_block(entry.ravel()), by_block(other.ravel()), by_block(entry_next)], 1),
        "entry_row": entry.ravel(),
        "wq": L0_gnn_Wq, "bq": L0_gnn_bq, "wk": L0_gnn_Wk, "bk": L0_gnn_bk, "wv": L0_gnn_Wv, "bv": L0_gnn_bv,
        "we": L0_gnn_We, "ws": L0_gnn_Ws, "bs": L0_gnn_bs,
    }
    arrays = {name: np.ascontiguousarray(a) for name, a in arrays.items()}
    nc = bacc.Bacc("TRN2", target_bir_lowering=False, num_devices=1)
    args = [nc.dram_tensor(f"{name}_dram", a.shape, mybir.dt.from_np(a.dtype), kind="ExternalInput").ap()
            for name, a in arrays.items()]
    out = nc.dram_tensor("out_dram", (NP, D), mybir.dt.from_np(x.dtype), kind="ExternalOutput").ap()
    build(nc, *args, out)
    r = run_bass_kernel_spmd(nc, [{f"{name}_dram": a for name, a in arrays.items()}], core_ids=[0])
    return r.results[0]["out_dram"][:N]
```

```python
from contextlib import ExitStack

import numpy as np

import concourse.bass as bass
from concourse import mybir

P = 128
D = 256
KC = D // P
H = 8
C = D // H
N = 50000
E = 25000

NG = 8
EG = 4
NODE_GROUPS = -(-N // (P * NG))
EDGE_GROUPS = -(-E // (P * EG))
NP = NODE_GROUPS * P * NG
TILES = EDGE_GROUPS * EG
EP = TILES * P
ENTRIES = 2 * TILES
EB = 4
EW = ENTRIES // EB
REC = 2 * D + 2 * H
SKIP = float(1 << 20)
FAR = 1.5e38
EPS = 1e-5
TINY = 1e-16
SCALE = float(C) ** -0.5

assert EDGE_GROUPS % 2 == 1 and NODE_GROUPS % 2 == 1 and ENTRIES % EB == 0 and EW <= P

ALU = mybir.AluOpType
ACT = mybir.ActivationFunctionType
AX = mybir.AxisListType
F32 = mybir.dt.float32
BF16 = mybir.dt.bfloat16
F32R = mybir.dt.float32r
I32 = mybir.dt.int32


def over(eng, sem, value):
    if not (isinstance(value, int) and value <= 0):
        eng.wait_ge(sem, value)


def apart(eng, passed, *waits):
    counts = [v if isinstance(v, int) else eng.lower_val(v) for _, v in waits]
    eng.wait_ge(*passed)
    for (sem, _), value in zip(waits, counts):
        over(eng, sem, value)


def wide(ap, n):
    return ap.unsqueeze(2).to_broadcast([ap.shape[0], ap.shape[1], n])


def build(nc, xt, xrows, et, slots, dst_row, flag_rows, cols, edge_ends, entry_cols, entry_row,
          wq, bq, wk, bk, wv, bv, we, ws, bs, out):
    bounds = nc.dram_tensor("bounds", [ENTRIES, REC], F32)
    with ExitStack() as ctx:
        def sb(name, shape, dt=F32):
            return ctx.enter_context(nc.sbuf_tensor(name, shape, dt))

        def sem(name):
            return ctx.enter_context(nc.semaphore(name))

        bank = [ctx.enter_context(nc.psum_tensor(f"bank{i}", [P, 512], F32)) for i in range(8)]

        ident = sb("ident", [P, P])
        ones = sb("ones", [P, P], BF16)
        half = sb("half", [P, NG])
        w_y = sb("w_y", [P, KC, D])
        w_kv = [sb(f"w_kv{i}", [P, KC, 2 * D], F32R) for i in range(2)]
        w_qs = [sb(f"w_qs{i}", [P, KC, 2 * D], F32R) for i in range(2)]
        w_e = [sb(f"w_e{i}", [P, KC, D], F32R) for i in range(2)]
        bias = sb("bias", [P, 4 * D])
        bias3 = sb("bias3", [P, 4 * D], BF16)
        mean = sb("mean", [P, KC + 1])
        flag = sb("flag", [EG * H, EDGE_GROUPS, P + 1])
        col_i = sb("col_i", [P, 2, TILES], I32)
        end_i = sb("end_i", [P, 2, TILES], I32)
        col_f = sb("col_f", [P, TILES])
        inner = sb("inner", [P, 3, TILES])
        where = sb("where", [P, TILES], I32)

        xT = [sb(f"xT{p}", [P, KC, NG, P]) for p in range(2)]
        y = [sb(f"y{p}", [P, NG, D]) for p in range(2)]
        square = [sb(f"square{i}", [P, D]) for i in range(2)]
        ssq = [sb(f"ssq{p}", [P, NG]) for p in range(2)]
        var = [sb(f"var{p}", [P, NG]) for p in range(2)]
        rstd = [sb(f"rstd{p}", [P, NG]) for p in range(2)]

        slot = [sb(f"slot{p}", [P, EG, 2], I32) for p in range(2)]
        goto = [sb(f"goto{p}", [P, EG], I32) for p in range(2)]
        eT = [sb(f"eT{h}", [P, 2 * KC * P]) for h in range(2)]
        e_part = [[sb(f"e_part{i}{h}", [P, 2, KC, P], F32R) for h in range(2)] for i in range(2)]
        dst_all = [sb(f"dst_all{p}", [P, EG * P], I32) for p in range(2)]
        rows_in = [sb(f"rows_in{j}", [P, 2, D]) for j in range(EG)]
        sdT = [[sb(f"sdT{i}{b}", [P, 2, KC, P], F32R) for b in range(2)] for i in range(2)]
        e_sb = [sb(f"e_sb{i}", [P, D]) for i in range(2)]
        qskv = sb("qskv", [P, 4, EG, 2 * D])
        qs = [qskv[:, p] for p in range(2)]
        kv = [qskv[:, 2 + p] for p in range(2)]
        prod = sb("prod", [P, D])
        alpha = [sb(f"alpha{p}", [P, EG * H]) for p in range(2)]
        same = [[sb(f"same{p}{j}", [P, P]) for j in range(EG)] for p in range(2)]
        at = sb("at", [EG * H, P + 1])
        run = sb("run", [EG * H, P])
        peak = sb("peak", [EG * H, P])
        below = sb("below", [P, EG * H])
        mv = sb("mv", [P, EG, D + H])
        dr = [sb(f"dr{p}", [P, EG, 2 * H]) for p in range(2)]
        den = sb("den", [P, EG * H])
        rden = sb("rden", [P, EG * H])
        avgz = sb("avgz", [P, 4, EG, D])
        avg = [avgz[:, p] for p in range(2)]
        z = [avgz[:, 2 + p] for p in range(2)]
        flag_i = qskv[0:EG * H].rearrange("p a j d -> p (a j d)")[:, 0:EDGE_GROUPS * P].bitcast(I32).rearrange(
            "p (g e) -> p g e", e=P)
        w_raw = avgz[:, 0:2]
        rest = avgz[:, 2].rearrange("p j d -> p (j d)")
        part = avgz[:, 3].rearrange("p j d -> p (j d)")[:, 0:2 * D].bitcast(BF16)
        stats = sb("stats", [P, EG, 6])
        moments = sb("moments", [P, EG, 2])
        vare = sb("vare", [P, EG])
        rstd2 = sb("rstd2", [P, EG])

        rec = sb("rec", [EW, EB, REC])
        ent_i = sb("ent_i", [EW, 3, EB], I32)
        ent_f = sb("ent_f", [EW, EB])
        erow_i = sb("erow_i", [P, ENTRIES], I32)
        eflag = sb("eflag", [H, ENTRIES + 1])
        esame = [xT[1][0:EW].rearrange("p c j n -> p (c j n)")[:, i * ENTRIES:(i + 1) * ENTRIES]
                 for i in range(EB)]
        erun, epeak = (xT[0][0:H].rearrange("p c j n -> p (c j n)")[:, i * ENTRIES:(i + 1) * ENTRIES]
                       for i in range(2))
        ebelow = sb("ebelow", [EW, EB * H])
        ep = sb("ep", [EW, EB * H])
        ekeep = sb("ekeep", [EW, EB])
        emv = y[0][0:EW].rearrange("p j d -> p (j d)")[:, 0:EB * (D + H)].rearrange("p (b w) -> p b w", b=EB)
        egoto = sb("egoto", [EW, EB], I32)
        enext = sb("enext", [EW, EB])
        eden = sb("eden", [EW, EB * H])
        erden = sb("erden", [EW, EB * H])
        ez = y[1][0:EW, 0:EB, :]
        estats = sb("estats", [EW, EB, 6])
        emoments = sb("emoments", [EW, EB, 2])
        evar = sb("evar", [EW, EB])
        erstd = sb("erstd", [EW, EB])

        loaded_y = sem("loaded_y")
        loaded_w = sem("loaded_w")
        loaded_i = sem("loaded_i")
        pool_const = sem("pool_const")
        step = sem("step")
        consts = sem("consts")
        x_in = [sem(f"x_in{p}") for p in range(2)]
        node_mm = sem("node_mm")
        biased = sem("biased")
        squared = sem("squared")
        var_ready = sem("var_ready")
        rstd_ready = sem("rstd_ready")
        node_rows = sem("node_rows")
        stored = [sem(f"stored{p}") for p in range(2)]

        slots_in = [sem(f"slots_in{p}") for p in range(2)]
        dst_in = [sem(f"dst_in{p}") for p in range(2)]
        e_in = [sem(f"e_in{h}") for h in range(2)]
        gathered = [sem(f"gathered{j}") for j in range(EG)]
        turned = sem("turned")
        high_ready = sem("high_ready")
        low_ready = sem("low_ready")
        e_high = sem("e_high")
        e_low = sem("e_low")
        prepared = sem("prepared")
        e_mm = sem("e_mm")
        kv_mm = sem("kv_mm")
        qs_mm = sem("qs_mm")
        e_copied = sem("e_copied")
        qs_copied = sem("qs_copied")
        kv_ready = sem("kv_ready")
        prod_ready = sem("prod_ready")
        alpha_ready = sem("alpha_ready")
        same_ready = sem("same_ready")
        alpha_turned = sem("alpha_turned")
        flag_ready = sem("flag_ready")
        run_ready = sem("run_ready")
        peak_ready = sem("peak_ready")
        peak_turned = sem("peak_turned")
        below_ready = sem("below_ready")
        peak_kept = sem("peak_kept")
        p_ready = sem("p_ready")
        mv_ready = sem("mv_ready")
        summed = sem("summed")
        den_ready = sem("den_ready")
        den_kept = sem("den_kept")
        rden_ready = sem("rden_ready")
        avg_ready = sem("avg_ready")
        z_ready = sem("z_ready")
        stats_ready = sem("stats_ready")
        moments_ready = sem("moments_ready")
        vare_ready = sem("vare_ready")
        rstd2_ready = sem("rstd2_ready")
        goto_ready = sem("goto_ready")
        edge_rows = sem("edge_rows")
        scattered = [sem(f"scattered{p}") for p in range(2)]
        y_kept = [sem(f"y_kept{p}") for p in range(2)]
        bound_out = [sem(f"bound_out{p}") for p in range(2)]

        rec_in = sem("rec_in")
        t_turned = sem("t_turned")
        t_step = sem("t_step")
        t_p = sem("t_p")
        t_mv = sem("t_mv")
        t_summed = sem("t_summed")
        t_var = sem("t_var")
        t_rstd = sem("t_rstd")
        t_rows = sem("t_rows")
        t_out = sem("t_out")

        turn_b, kv_b, qs_b, e_b, sum_b, small_b = bank[0], bank[1:3], bank[3], bank[4], bank[5:7], bank[7]
        aT_ps = small_b[0:EG * H, 0:P]
        peak_ps = small_b[:, P:P + EG * H]
        den_ps = small_b[:, P + EG * H:P + 2 * EG * H]

        out_groups = out.rearrange("(g p j) d -> g p j d", p=P, j=NG)
        bound_rows = bounds.ap().rearrange("(t r) w -> r t w", r=2)
        NODE_PAIRS = NG // 2
        BOUND_DMAS = 2
        GO_LAST = EDGE_GROUPS - 1

        def groups(eng, body, last):
            for g in range(4):
                body(g, g % 2, g // 2)
            with eng.Fori(0, (last - 4) // 2) as m:
                body(m * 2 + 4, 0, m + 2)
                body(m * 2 + 5, 1, m + 2)
            body(last, 0, last // 2)

        def node_groups(eng, body):
            groups(eng, body, NODE_GROUPS - 1)

        def edge_groups(eng, body):
            groups(eng, body, GO_LAST)

        def is_first(g):
            return isinstance(g, int) and g == 0

        def is_early(g):
            return isinstance(g, int) and g < 2

        def is_last(g):
            return isinstance(g, int) and g == GO_LAST

        block = ctx.enter_context(nc.Block())

        @block.sync
        def _(sp):
            sp.dma_start(w_y[:], ws.rearrange("(c k) n -> k c n", k=P)).then_inc(loaded_y, 16)
            for i, b in enumerate((bk, bv, bq, bs)):
                sp.dma_start(bias[:, i * D:(i + 1) * D], b.partition_broadcast(P)).then_inc(loaded_y, 16)

            def load_rest():
                for i, w in enumerate((wk, wv, wq, we)):
                    sp.dma_start(w_raw[:, :, i, :], w.rearrange("(c k) n -> k c n", k=P)).then_inc(loaded_w, 16)
                sp.dma_start(col_i[:], cols).then_inc(loaded_i, 16)
                for i in range(2):
                    sp.dma_start(end_i[:, i, :], edge_ends[i].partition_broadcast(P)).then_inc(loaded_i, 16)
                for j in range(EG):
                    sp.dma_start(flag_i[j * H:(j + 1) * H].rearrange("h g e -> h (g e)"),
                                 flag_rows[j].partition_broadcast(H)).then_inc(loaded_i, 16)
                sp.dma_start(ent_i[:], entry_cols).then_inc(loaded_i, 16)
                sp.dma_start(erow_i[:], entry_row.partition_broadcast(P)).then_inc(loaded_i, 16)

            def load_x(g, par, u):
                over(sp, node_mm, (g - 1) * NODE_PAIRS)
                sp.dma_start(xT[par][:], xt[g]).then_inc(x_in[par], 16)
                if isinstance(g, int) and g == 1:
                    load_rest()

            node_groups(sp, load_x)

            def load_numbers(g, par):
                over(sp, turned, (g - 1) * EG)
                sp.dma_start(slot[par][:], slots[g]).then_inc(slots_in[par], 16)
                over(sp, same_ready, (g - 1) * EG)
                sp.dma_start(dst_all[par][:], dst_row[g].partition_broadcast(P)).then_inc(dst_in[par], 16)

            def load_e(g, h):
                over(sp, e_low, g * 2 + h - 1)
                sp.dma_start(eT[h][:], et[g * 2 + h]).then_inc(e_in[h], 16)

            def keep_y(g, par):
                apart(sp, (x_in[0], 16), (qs_copied, (g + 1) * EG))
                sp.dma_start(bound_rows[:, bass.ds(g * EG, EG), D:2 * D],
                             qs[par][0:P:P - 1, :, D:]).then_inc(y_kept[par], 16)

            def keep_bounds(g, par, u):
                apart(sp, (x_in[0], 16), (avg_ready, g * 2 + 2), (peak_kept, g + 1), (den_kept, g + 1))
                ends = slice(0, P, P - 1)
                table = bound_rows[:, bass.ds(g * EG, EG), :]
                sp.dma_start(table[:, :, 0:D], avg[par][ends]).then_inc(bound_out[par], 16)
                sp.dma_start(table[:, :, 2 * D:], dr[par][ends, :, :]).then_inc(bound_out[par], 16)

            load_numbers(0, 0)
            load_e(0, 0)
            load_e(0, 1)

            def edge_body(g, par, u):
                if not is_first(g):
                    keep_y(g - 1, 1 - par)
                if not is_last(g):
                    load_numbers(g + 1, 1 - par)
                    load_e(g + 1, 0)
                if not is_early(g):
                    keep_bounds(g - 2, par, u - 1)
                if not is_last(g):
                    load_e(g + 1, 1)

            edge_groups(sp, edge_body)
            keep_y(GO_LAST, 0)
            keep_bounds(GO_LAST - 1, 1, 0)
            keep_bounds(GO_LAST, 0, 0)
            sp.wait_ge(bound_out[0], 16 * BOUND_DMAS * (GO_LAST // 2 + 1))
            sp.wait_ge(bound_out[1], 16 * BOUND_DMAS * (GO_LAST // 2))
            sp.wait_ge(y_kept[0], 16 * (GO_LAST // 2 + 1))
            sp.wait_ge(y_kept[1], 16 * (GO_LAST // 2))
            sp.dma_start(rec[:], bounds.ap().rearrange("(b i) w -> i b w", b=EB)).then_inc(rec_in, 16)
            sp.wait_ge(stored[0], 16 * (NODE_GROUPS // 2 + 1))
            sp.wait_ge(stored[1], 16 * (NODE_GROUPS // 2))
            sp.wait_ge(scattered[0], 16 * EG * (GO_LAST // 2 + 1))
            sp.wait_ge(scattered[1], 16 * EG * (GO_LAST // 2))
            sp.wait_ge(t_out, 16 * EB)

        @block.gpsimd
        def _(pool):
            nc.gpsimd.memset(ident[:], 0.0).then_inc(pool_const, 1)
            pool.wait_ge(pool_const, 1)
            nc.gpsimd.affine_select(out=ident[:], in_=ident[:], compare_op=ALU.not_equal, fill=1.0, base=0,
                                    pattern=[[-1, P]], channel_multiplier=1).then_inc(pool_const, 1)
            nc.gpsimd.memset(ones[:], 1.0).then_inc(pool_const, 1)
            nc.gpsimd.memset(half[:], -0.5).then_inc(pool_const, 1)
            pool.wait_ge(pool_const, 4)

            def nodes(g, par, u):
                pool.wait_ge(var_ready, g + 1)
                nc.gpsimd.tensor_tensor(rstd[par][:], var[par][:], half[:], ALU.pow).then_inc(rstd_ready, 1)
                pool.wait_ge(node_rows, g + 1)
                pool.dma_start(out_groups[g], y[par][:]).then_inc(stored[par], 16)

            node_groups(pool, nodes)
            pool.wait_ge(stored[0], 16 * (NODE_GROUPS // 2 + 1))
            pool.wait_ge(stored[1], 16 * (NODE_GROUPS // 2))

            def gather(g, par, u, j):
                apart(pool, (pool_const, 4), (turned, (g - 1) * EG + j + 1),
                      *[(slots_in[par], (u + 1) * 16)] * (j == 0))
                for i in range(2):
                    nc.gpsimd.indirect_dma_start(
                        out=rows_in[j][:, i, :], out_offset=None, in_=xrows,
                        in_offset=bass.IndirectOffsetOnAxis(ap=slot[par][:, j, i:i + 1], axis=0),
                    ).then_inc(gathered[j], 16)

            def add_y(g, par, u, b):
                pool.wait_ge(avg_ready, g * 2 + b + 1)
                if b == 0:
                    over(pool, scattered[par], u * 16 * EG)
                for j in (2 * b, 2 * b + 1):
                    ins = nc.gpsimd.tensor_tensor(z[par][:, j, :], avg[par][:, j, :], qs[par][:, j, D:], ALU.add)
                ins.then_inc(z_ready, 1)

            def root(g):
                pool.wait_ge(vare_ready, g + 1)
                nc.gpsimd.tensor_tensor(rstd2[:], vare[:], half[:, 0:EG], ALU.pow).then_inc(rstd2_ready, 1)

            def scatter(g, par, u):
                apart(pool, (pool_const, 4), (edge_rows, g + 1), (goto_ready, g + 1))
                for j in range(EG):
                    nc.gpsimd.indirect_dma_start(
                        out=out, out_offset=bass.IndirectOffsetOnAxis(ap=goto[par][:, j:j + 1], axis=0),
                        in_=z[par][:, j, :], in_offset=None, bounds_check=NP - 1, oob_is_err=False,
                    ).then_inc(scattered[par], 16)

            def finish(g, par, u, more):
                add_y(g, par, u, 0)
                add_y(g, par, u, 1)
                more(2)
                root(g)
                more(3)
                scatter(g, par, u)

            for j in range(EG):
                gather(0, 0, 0, j)

            def edge_body(g, par, u):
                def more(j):
                    if not is_last(g):
                        gather(g + 1, 1 - par, u + par, j)
                more(0)
                more(1)
                if is_early(g):
                    more(2)
                    more(3)
                else:
                    finish(g - 2, par, u - 1, more)

            edge_groups(pool, edge_body)
            finish(GO_LAST - 1, 1, GO_LAST // 2 - 1, lambda j: None)
            finish(GO_LAST, 0, GO_LAST // 2, lambda j: None)

            pool.wait_ge(t_var, 1)
            nc.gpsimd.tensor_tensor(erstd[:], evar[:], half[0:EW, 0:EB], ALU.pow).then_inc(t_rstd, 1)
            pool.wait_ge(t_rows, 1)
            for b in range(EB):
                nc.gpsimd.indirect_dma_start(
                    out=out, out_offset=bass.IndirectOffsetOnAxis(ap=egoto[:, b:b + 1], axis=0),
                    in_=ez[:, b, :], in_offset=None, bounds_check=NP - 1, oob_is_err=False,
                ).then_inc(t_out, 16)

        @block.scalar
        def _(act):
            def nodes(g, par, u):
                over(act, var_ready, g - 1)
                for b in range(NODE_PAIRS):
                    act.wait_ge(biased, g * NODE_PAIRS + b + 1)
                    for j in (2 * b, 2 * b + 1):
                        over(act, squared, g * NG + j - 1)
                        nc.scalar.activation(square[j % 2][:], y[par][:, j, :], ACT.Square,
                                             accum_out=ssq[par][:, j:j + 1]).then_inc(squared, 1)

            node_groups(act, nodes)

            def high(g, j):
                t = g * EG + j
                act.wait_ge(turned, t + 1)
                over(act, qs_mm, t - 1)
                nc.scalar.copy(sdT[0][j % 2][:].rearrange("p a c e -> p (a c e)"), turn_b[:]).then_inc(high_ready, 1)

            def high_e(g, h):
                act.wait_ge(e_in[h], (g + 1) * 16)
                over(act, e_mm, (g - 1) * EG + 2 * h + 2)
                nc.scalar.copy(e_part[0][h][:].rearrange("p j c e -> p (j c e)"), eT[h][:]).then_inc(e_high, 1)

            def tile(g, par, u, j):
                t = g * EG + j
                if not (is_last(g) and j == EG - 1):
                    high(g, j + 1) if j < EG - 1 else high(g + 1, 0)
                if j == 1:
                    high_e(g, 1)
                if j == EG - 1 and not is_last(g):
                    high_e(g + 1, 0)
                act.wait_ge(e_mm, t + 1)
                over(act, kv_ready, t - 1)
                nc.scalar.copy(e_sb[j % 2][:], e_b[:, 0:D]).then_inc(e_copied, 1)
                if j == 2 and not is_first(g):
                    weigh(g - 1)
                act.wait_ge(qs_mm, t + 1)
                if j % 2 == 0:
                    over(act, z_ready, (g - 2) * 2 + j // 2 + 1)
                if j == 0:
                    over(act, y_kept[par], u * 16)
                nc.scalar.copy(qs[par][:, j], qs_b[:]).then_inc(qs_copied, 1)

            def weigh(g):
                act.wait_ge(below_ready, g + 1)
                over(act, summed, g)
                nc.scalar.activation(mv[:, :, D:], below[:].rearrange("p (j h) -> p j h", h=H), ACT.Exp,
                                     scale=SCALE).then_inc(p_ready, 1)

            act.wait_ge(squared, NODE_GROUPS * NG)
            high_e(0, 0)
            high(0, 0)

            def edge_body(g, par, u):
                for j in range(EG):
                    tile(g, par, u, j)

            edge_groups(act, edge_body)
            weigh(GO_LAST)
            act.wait_ge(t_step, 4)
            nc.scalar.activation(ep[:], ebelow[:], ACT.Exp, scale=SCALE).then_inc(t_p, 1)

        @block.vector
        def _(dve):
            made = [0]

            def then(ins):
                made[0] += 1
                ins.then_inc(step, 1)
                dve.wait_ge(step, made[0])

            dve.wait_ge(loaded_y, 16 * 5)
            dve.wait_ge(pool_const, 4)
            for c in range(KC):
                diag = w_y[:, c, c * P:(c + 1) * P]
                then(nc.vector.tensor_tensor(diag, diag, ident[:], ALU.add))
            then(nc.vector.tensor_reduce(mean[:, 0:KC], w_y[:], AX.X, ALU.add))
            then(nc.vector.tensor_reduce(mean[:, KC:], bias[:, 3 * D:], AX.X, ALU.add))
            then(nc.vector.tensor_scalar(mean[:], mean[:], 1.0 / D, None, ALU.mult))
            for c in range(KC):
                then(nc.vector.tensor_scalar(w_y[:, c], w_y[:, c], mean[:, c:c + 1], None, ALU.subtract))
            then(nc.vector.tensor_scalar(bias[:, 3 * D:], bias[:, 3 * D:], mean[:, KC:], None, ALU.subtract))
            nc.vector.engine_nop().then_inc(consts, 1)

            def split_weights():
                dve.wait_ge(loaded_w, 16 * 4)
                for parts, n, w in ((w_kv, 0, w_raw[:, :, 0]), (w_kv, 1, w_raw[:, :, 1]), (w_qs, 0, w_raw[:, :, 2]),
                                    (w_qs, 1, w_y[:]), (w_e, 0, w_raw[:, :, 3])):
                    hi, lo = (a[:, :, n * D:(n + 1) * D] for a in parts)
                    then(nc.vector.tensor_copy(hi, w))
                    then(nc.vector.tensor_tensor(lo, w, hi.bitcast(F32), ALU.subtract))

            def split_biases():
                then(nc.vector.tensor_copy(rest, bias[:]))
                for i in range(3):
                    then(nc.vector.tensor_copy(part, rest))
                    if i == 0:
                        then(nc.vector.tensor_scalar(bias3[:], part, ident[:, 0:1], None, ALU.mult))
                    else:
                        then(nc.vector.scalar_tensor_tensor(out=bias3[:], in0=part, scalar=ident[:, i:i + 1],
                                                            in1=bias3[:], op0=ALU.mult, op1=ALU.add))
                    if i < 2:
                        then(nc.vector.tensor_tensor(rest, rest, part, ALU.subtract))

            def nodes(g, par, u):
                over(dve, stored[par], u * 16)
                for b in range(NODE_PAIRS):
                    dve.wait_ge(node_mm, g * NODE_PAIRS + b + 1)
                    nc.vector.tensor_tensor(
                        y[par][:, 2 * b:2 * b + 2, :],
                        bank[par * NODE_PAIRS + b][:].rearrange("p (j d) -> p j d", j=2),
                        bias[:, 3 * D:].unsqueeze(1).to_broadcast([P, 2, D]), ALU.add).then_inc(biased, 1)
                dve.wait_ge(squared, (g + 1) * NG)
                over(dve, rstd_ready, g - 1)
                nc.vector.tensor_scalar(var[par][:], ssq[par][:], 1.0 / D, EPS, ALU.mult, ALU.add).then_inc(var_ready, 1)
                dve.wait_ge(rstd_ready, g + 1)
                for j in range(NG):
                    ins = nc.vector.tensor_scalar(y[par][:, j, :], y[par][:, j, :], rstd[par][:, j:j + 1],
                                                  None, ALU.mult)
                ins.then_inc(node_rows, 1)

            def mark_segments():
                dve.wait_ge(loaded_i, 16 * (1 + 2 + EG + 2))
                nc.vector.memset(flag[:, :, 0:1], -FAR)
                nc.vector.memset(flag[:, :, P:P + 1], -FAR)
                then(nc.vector.tensor_tensor(flag[:, :, 1:P], flag_i[:, :, 1:P], flag_i[:, :, 0:P - 1], ALU.not_equal))
                then(nc.vector.tensor_scalar(flag[:, :, 1:P], flag[:, :, 1:P], -FAR, None, ALU.mult))
                then(nc.vector.tensor_copy(col_f[:], col_i[:, 0, :]))
                then(nc.vector.tensor_tensor(inner[:, 0, :], col_i[:, 0, :], col_i[:, 1, :], ALU.is_equal))
                then(nc.vector.tensor_tensor(inner[:, 1, :], col_i[:, 0, :], end_i[:, 0, :], ALU.is_equal))
                then(nc.vector.tensor_tensor(inner[:, 2, :], col_i[:, 0, :], end_i[:, 1, :], ALU.is_equal))
                then(nc.vector.tensor_tensor(inner[:, 0, :], inner[:, 0, :], inner[:, 1, :], ALU.max))
                then(nc.vector.tensor_tensor(inner[:, 0, :], inner[:, 0, :], inner[:, 2, :], ALU.max))
                then(nc.vector.scalar_tensor_tensor(out=where[:], in0=inner[:, 0, :], scalar=SKIP, in1=col_f[:],
                                                    op0=ALU.mult, op1=ALU.add))

            def nodes_and_rest(g, par, u):
                nodes(g, par, u)
                if isinstance(g, int) and g < 3:
                    (split_weights, split_biases, mark_segments)[g]()
                    if g == 2:
                        nc.vector.engine_nop().then_inc(prepared, 1)

            node_groups(dve, nodes_and_rest)

            def low(g, j):
                t = g * EG + j
                dve.wait_ge(high_ready, t + 1)
                nc.vector.tensor_tensor(sdT[1][j % 2][:].rearrange("p a c e -> p (a c e)"), turn_b[:],
                                        sdT[0][j % 2][:].rearrange("p a c e -> p (a c e)").bitcast(F32),
                                        ALU.subtract).then_inc(low_ready, 1)

            def low_e(g, h):
                dve.wait_ge(e_high, g * 2 + h + 1)
                nc.vector.tensor_tensor(e_part[1][h][:].rearrange("p j c e -> p (j c e)"), eT[h][:],
                                        e_part[0][h][:].rearrange("p j c e -> p (j c e)").bitcast(F32),
                                        ALU.subtract).then_inc(e_low, 1)

            def tile(g, par, u, j):
                t = g * EG + j
                if not (is_last(g) and j == EG - 1):
                    low(g, j + 1) if j < EG - 1 else low(g + 1, 0)
                if j == 1:
                    low_e(g, 1)
                if j == EG - 1 and not is_last(g):
                    low_e(g + 1, 0)
                dve.wait_ge(kv_mm, t + 1)
                dve.wait_ge(e_copied, t + 1)
                if j == 0:
                    over(dve, mv_ready, g - 1)
                nc.vector.tensor_tensor(kv[par][:, j].rearrange("p (a d) -> p a d", a=2),
                                        kv_b[j % 2][:].rearrange("p (a d) -> p a d", a=2),
                                        e_sb[j % 2][:].unsqueeze(1).to_broadcast([P, 2, D]),
                                        ALU.add).then_inc(kv_ready, 1)
                if j == 0:
                    dve.wait_ge(dst_in[par], (u + 1) * 16)
                    over(dve, summed, g - 1)
                nc.vector.tensor_scalar(same[par][j][:], dst_all[par][:, j * P:(j + 1) * P],
                                        col_f[:, bass.ds(t, 1)], None, ALU.is_equal).then_inc(same_ready, 1)
                dve.wait_ge(qs_copied, t + 1)
                dve.wait_ge(kv_ready, t + 1)
                over(dve, alpha_ready, t)
                nc.vector.tensor_tensor(prod[:], kv[par][:, j, 0:D], qs[par][:, j, 0:D],
                                        ALU.mult).then_inc(prod_ready, 1)
                dve.wait_ge(prod_ready, t + 1)
                if j == 0:
                    over(dve, alpha_turned, g - 1)
                    over(dve, below_ready, g - 1)
                nc.vector.tensor_reduce(alpha[par][:, j * H:(j + 1) * H],
                                        prod[:].rearrange("p (h c) -> p h c", h=H), AX.X,
                                        ALU.add).then_inc(alpha_ready, 1)

            def maxima(g):
                over(dve, peak_ready, g)
                nc.vector.tensor_copy(at[:], flag[:, bass.ds(g, 1), :].rearrange("p o e -> p (o e)")).then_inc(flag_ready, 1)
                dve.wait_ge(flag_ready, g + 1)
                dve.wait_ge(alpha_turned, g + 1)
                nc.vector.tensor_tensor_scan(run[:], at[:, 0:P], aT_ps, -FAR, ALU.add, ALU.max).then_inc(run_ready, 1)
                dve.wait_ge(run_ready, g + 1)
                over(dve, peak_turned, g)
                nc.vector.tensor_tensor_scan(peak[:, ::-1], at[:, 1:P + 1][:, ::-1], run[:, ::-1], -FAR,
                                             ALU.add, ALU.max).then_inc(peak_ready, 1)

            def shift(g, par, u):
                dve.wait_ge(peak_turned, g + 1)
                over(dve, p_ready, g)
                nc.vector.tensor_tensor(below[:], alpha[par][:], peak_ps, ALU.subtract).then_inc(below_ready, 1)
                over(dve, bound_out[par], u * 16 * BOUND_DMAS)
                nc.vector.tensor_copy(dr[par][:, :, H:], peak_ps.rearrange("p (j h) -> p j h", h=H)).then_inc(peak_kept, 1)

            def weigh(g, par):
                dve.wait_ge(p_ready, g + 1)
                over(dve, summed, g)
                for j in range(EG):
                    ins = nc.vector.tensor_tensor(
                        mv[:, j, 0:D].rearrange("p (h c) -> p h c", h=H),
                        kv[par][:, j, D:].rearrange("p (h c) -> p h c", h=H),
                        wide(mv[:, j, D:], C), ALU.mult)
                ins.then_inc(mv_ready, 1)

            def average(g, par, u):
                dve.wait_ge(summed, g + 1)
                over(dve, rden_ready, g)
                nc.vector.tensor_scalar(den[:], den_ps, TINY, None, ALU.add).then_inc(den_ready, 1)
                nc.vector.tensor_copy(dr[par][:, :, 0:H], den_ps.rearrange("p (j h) -> p j h", h=H)).then_inc(den_kept, 1)
                dve.wait_ge(den_ready, g + 1)
                over(dve, avg_ready, g * 2)
                nc.vector.reciprocal(rden[:], den[:]).then_inc(rden_ready, 1)
                dve.wait_ge(rden_ready, g + 1)
                over(dve, bound_out[par], u * 16 * BOUND_DMAS)
                for b in range(2):
                    nc.vector.tensor_tensor(
                        avg[par][:, 2 * b:2 * b + 2, :].rearrange("p j (h c) -> p (j h) c", h=H),
                        sum_b[b][:].rearrange("p (h c) -> p h c", c=C),
                        wide(rden[:, 2 * b * H:(2 * b + 2) * H], C), ALU.mult).then_inc(avg_ready, 1)

            def spread(g, par):
                dve.wait_ge(z_ready, g * 2 + 2)
                over(dve, moments_ready, g)
                for j in range(EG):
                    ins = nc.vector.bn_stats(stats[:, j, :], z[par][:, j, :])
                ins.then_inc(stats_ready, 1)
                apart(dve, (pool_const, 4), (stats_ready, g + 1), (edge_rows, g))
                for j in range(EG):
                    ins = nc.vector.bn_aggr(moments[:, j, :], stats[:, j, :])
                ins.then_inc(moments_ready, 1)
                dve.wait_ge(moments_ready, g + 1)
                over(dve, rstd2_ready, g)
                nc.vector.tensor_scalar(vare[:], moments[:, :, 1], EPS, None, ALU.add).then_inc(vare_ready, 1)

            def rows(g, par, u):
                over(dve, scattered[par], u * 16 * EG)
                nc.vector.tensor_copy(goto[par][:], where[:, bass.ds(g * EG, EG)]).then_inc(goto_ready, 1)
                dve.wait_ge(rstd2_ready, g + 1)
                for j in range(EG):
                    ins = nc.vector.tensor_scalar(z[par][:, j, :], z[par][:, j, :], moments[:, j, 0:1],
                                                  rstd2[:, j:j + 1], ALU.subtract, ALU.mult)
                ins.then_inc(edge_rows, 1)

            low_e(0, 0)
            low(0, 0)

            def edge_body(g, par, u):
                if not is_early(g):
                    average(g - 2, par, u - 1)
                tile(g, par, u, 0)
                if not is_first(g):
                    maxima(g - 1)
                tile(g, par, u, 1)
                if not is_first(g):
                    shift(g - 1, 1 - par, u - 1 + par)
                if not is_early(g):
                    spread(g - 2, par)
                tile(g, par, u, 2)
                if not is_first(g):
                    weigh(g - 1, 1 - par)
                if not is_early(g):
                    rows(g - 2, par, u - 1)
                tile(g, par, u, 3)

            edge_groups(dve, edge_body)
            last_u = GO_LAST // 2
            average(GO_LAST - 1, 1, last_u - 1)
            maxima(GO_LAST)
            shift(GO_LAST, 0, last_u)
            weigh(GO_LAST, 0)
            spread(GO_LAST - 1, 1)
            rows(GO_LAST - 1, 1, last_u - 1)
            average(GO_LAST, 0, last_u)
            spread(GO_LAST, 0)
            rows(GO_LAST, 0, last_u)

            t_made = [0]

            def t_then(ins):
                t_made[0] += 1
                ins.then_inc(t_step, 1)
                dve.wait_ge(t_step, t_made[0])

            nc.vector.memset(eflag[:, 0:1], -FAR)
            nc.vector.memset(eflag[:, ENTRIES:], -FAR)
            then(nc.vector.tensor_tensor(eflag[:, 1:ENTRIES], erow_i[0:H, 1:], erow_i[0:H, 0:ENTRIES - 1], ALU.not_equal))
            then(nc.vector.tensor_scalar(eflag[:, 1:ENTRIES], eflag[:, 1:ENTRIES], -FAR, None, ALU.mult))
            then(nc.vector.tensor_copy(ent_f[:], ent_i[:, 0, :]))
            then(nc.vector.tensor_tensor(ekeep[:], ent_i[:, 0, :], ent_i[:, 1, :], ALU.not_equal))
            then(nc.vector.tensor_tensor(enext[:], ent_i[:, 0, :], ent_i[:, 2, :], ALU.is_equal))
            then(nc.vector.scalar_tensor_tensor(out=egoto[:], in0=enext[:], scalar=SKIP, in1=ent_f[:],
                                                op0=ALU.mult, op1=ALU.add))
            for i in range(EB):
                ins = nc.vector.tensor_scalar(esame[i], erow_i[0:EW, :], ent_f[:, i:i + 1], None, ALU.is_equal)
            then(ins)
            dve.wait_ge(t_turned, 1)
            t_then(nc.vector.tensor_tensor_scan(erun, eflag[:, 0:ENTRIES], kv_b[0][0:H, 0:ENTRIES], -FAR,
                                                ALU.add, ALU.max))
            t_then(nc.vector.tensor_tensor_scan(epeak[:, ::-1], eflag[:, 1:][:, ::-1], erun[:, ::-1], -FAR,
                                                ALU.add, ALU.max))
            dve.wait_ge(t_turned, 2)
            dve.wait_ge(rec_in, 16)
            t_then(nc.vector.tensor_tensor(ebelow[:].rearrange("p (b h) -> p b h", h=H), rec[:, :, 2 * D + H:],
                                           kv_b[1][0:EW, 0:EB * H].rearrange("p (b h) -> p b h", h=H), ALU.subtract))
            t_then(nc.vector.tensor_tensor(emv[:, :, D:], rec[:, :, 2 * D:2 * D + H], wide(ekeep[:], H), ALU.mult))
            dve.wait_ge(t_p, 1)
            t_then(nc.vector.tensor_tensor(emv[:, :, D:], emv[:, :, D:], ep[:].rearrange("p (b h) -> p b h", h=H), ALU.mult))
            for b in range(EB):
                ins = nc.vector.tensor_tensor(emv[:, b, 0:D].rearrange("p (h c) -> p h c", h=H),
                                              rec[:, b, 0:D].rearrange("p (h c) -> p h c", h=H),
                                              wide(emv[:, b, D:], C), ALU.mult)
            ins.then_inc(t_mv, 1)
            for b in range(EB):
                dve.wait_ge(t_summed, b + 1)
                t_then(nc.vector.tensor_scalar(eden[:, b * H:(b + 1) * H], bank[3 + b][0:EW, D:D + H], TINY, None, ALU.add))
                t_then(nc.vector.reciprocal(erden[:, b * H:(b + 1) * H], eden[:, b * H:(b + 1) * H]))
                t_then(nc.vector.tensor_tensor(ez[:, b, :].rearrange("p (h c) -> p h c", h=H),
                                               bank[3 + b][0:EW, 0:D].rearrange("p (h c) -> p h c", h=H),
                                               wide(erden[:, b * H:(b + 1) * H], C), ALU.mult))
                t_then(nc.vector.tensor_tensor(ez[:, b, :], ez[:, b, :], rec[:, b, D:2 * D], ALU.add))
                t_then(nc.vector.bn_stats(estats[:, b, :], ez[:, b, :]))
                t_then(nc.vector.bn_aggr(emoments[:, b, :], estats[:, b, :]))
            nc.vector.tensor_scalar(evar[:], emoments[:, :, 1], EPS, None, ALU.add).then_inc(t_var, 1)
            dve.wait_ge(t_rstd, 1)
            for b in range(EB):
                ins = nc.vector.tensor_scalar(ez[:, b, :], ez[:, b, :], emoments[:, b, 0:1], erstd[:, b:b + 1],
                                              ALU.subtract, ALU.mult)
            ins.then_inc(t_rows, 1)

        @block.tensor
        def _(pe):
            pe.wait_ge(consts, 1)

            def nodes(g, par, u):
                pe.wait_ge(x_in[par], (u + 1) * 16)
                for b in range(NODE_PAIRS):
                    over(pe, biased, (g - 2) * NODE_PAIRS + b + 1)
                    for i in range(2):
                        for c in range(KC):
                            ins = nc.tensor.matmul(bank[par * NODE_PAIRS + b][:, i * D:(i + 1) * D],
                                                   xT[par][:, c, 2 * b + i, :], w_y[:, c, :],
                                                   start=(c == 0), stop=(c == KC - 1))
                    ins.then_inc(node_mm, 1)

            node_groups(pe, nodes)
            pe.wait_ge(biased, NODE_GROUPS * NODE_PAIRS)

            def turn(g, j):
                t = g * EG + j
                pe.wait_ge(gathered[j], (g + 1) * 32)
                over(pe, low_ready, t)
                for i in range(2):
                    for c in range(KC):
                        ins = nc.tensor.transpose(turn_b[:, (i * KC + c) * P:(i * KC + c + 1) * P],
                                                  rows_in[j][:, i, c * P:(c + 1) * P], ident[:])
                ins.then_inc(turned, 1)

            def product(to, rows, weights, first):
                terms = [(c, a, b) for c in range(KC) for a, b in ((0, 0), (0, 1), (1, 0))]
                for n, (c, a, b) in enumerate(terms):
                    ins = nc.tensor.matmul(to, rows[a][:, c, :], weights[b][:, c, :],
                                           start=(first and n == 0), stop=(n == len(terms) - 1))
                return ins

            def tile(g, par, u, j):
                t = g * EG + j
                if not (is_last(g) and j == EG - 1):
                    turn(g, j + 1) if j < EG - 1 else turn(g + 1, 0)
                if j % 2 == 0:
                    pe.wait_ge(e_low, g * 2 + j // 2 + 1)
                over(pe, e_copied, t)
                product(e_b[:, 0:D], [a[j // 2][:, j % 2] for a in e_part], w_e, True).then_inc(e_mm, 1)
                pe.wait_ge(low_ready, t + 1)
                over(pe, kv_ready, t - 1)
                nc.tensor.matmul(kv_b[j % 2][:], ones[:], bias3[:, 0:2 * D], start=True, stop=False)
                product(kv_b[j % 2][:], [a[j % 2][:, 0] for a in sdT], w_kv, False).then_inc(kv_mm, 1)
                over(pe, qs_copied, t)
                nc.tensor.matmul(qs_b[:], ones[:], bias3[:, 2 * D:], start=True, stop=False)
                product(qs_b[:], [a[j % 2][:, 1] for a in sdT], w_qs, False).then_inc(qs_mm, 1)

            def turn_alpha(g, par):
                pe.wait_ge(alpha_ready, (g + 1) * EG)
                over(pe, den_kept, g)
                nc.tensor.transpose(aT_ps, alpha[par][:], ident[:]).then_inc(alpha_turned, 1)

            def turn_peak(g):
                apart(pe, (consts, 1), (peak_ready, g + 1))
                nc.tensor.transpose(peak_ps, peak[:], ident[0:EG * H, 0:EG * H]).then_inc(peak_turned, 1)

            def add_up(g, par):
                pe.wait_ge(mv_ready, g + 1)
                pe.wait_ge(peak_kept, g + 1)
                pe.wait_ge(same_ready, (g + 1) * EG)
                over(pe, avg_ready, g * 2)
                for j in range(EG):
                    nc.tensor.matmul(sum_b[j // 2][:, (j % 2) * D:(j % 2 + 1) * D], same[par][j][:],
                                     mv[:, j, 0:D], start=True, stop=True)
                    ins = nc.tensor.matmul(den_ps[:, j * H:(j + 1) * H], same[par][j][:], mv[:, j, D:],
                                           start=True, stop=True)
                ins.then_inc(summed, 1)

            pe.wait_ge(prepared, 1)
            turn(0, 0)

            def edge_body(g, par, u):
                tile(g, par, u, 0)
                if not is_first(g):
                    turn_alpha(g - 1, 1 - par)
                tile(g, par, u, 1)
                if not is_first(g):
                    turn_peak(g - 1)
                tile(g, par, u, 2)
                tile(g, par, u, 3)
                if not is_first(g):
                    add_up(g - 1, 1 - par)

            edge_groups(pe, edge_body)
            turn_alpha(GO_LAST, 0)
            turn_peak(GO_LAST)
            add_up(GO_LAST, 0)

            pe.wait_ge(rec_in, 16)
            for b in range(EB):
                ins = nc.tensor.transpose(kv_b[0][0:H, b * EW:(b + 1) * EW], rec[:, b, 2 * D + H:],
                                          ident[0:EW, 0:EW])
            ins.then_inc(t_turned, 1)
            pe.wait_ge(t_step, 2)
            for b in range(EB):
                ins = nc.tensor.transpose(kv_b[1][0:EW, b * H:(b + 1) * H], epeak[:, b * EW:(b + 1) * EW],
                                          ident[0:H, 0:H])
            ins.then_inc(t_turned, 1)
            pe.wait_ge(t_mv, 1)
            pe.wait_ge(avg_ready, 2 * EDGE_GROUPS)
            for b in range(EB):
                for i in range(EB):
                    ins = nc.tensor.matmul(bank[3 + b][0:EW, 0:D + H], esame[i][:, b * EW:(b + 1) * EW],
                                           emv[:, i, :], start=(i == 0), stop=(i == EB - 1))
                ins.then_inc(t_summed, 1)

    return nc


def kernel(x, src, dst, edge_attr_256, L0_gnn_Wq, L0_gnn_bq, L0_gnn_Wk, L0_gnn_bk, L0_gnn_Wv, L0_gnn_bv,
           L0_gnn_We, L0_gnn_Ws, L0_gnn_bs):
    import concourse.bacc as bacc
    from concourse.bass_utils import run_bass_kernel_spmd

    x, src, dst, ea = (np.asarray(a) for a in (x, src, dst, edge_attr_256))
    xp = np.zeros((NP, D), x.dtype)
    xp[:N] = x
    ep = np.zeros((EP, D), ea.dtype)
    ep[:E] = ea
    sp = np.zeros(EP, src.dtype)
    sp[:E] = src
    dp = np.full(EP, N, dst.dtype)
    dp[:E] = dst

    tiles = dp.reshape(TILES, P)
    nxt = np.concatenate([dp[1:], dp[-1:]]).reshape(TILES, P)
    entry = tiles[:, [0, P - 1]]
    other = np.stack([np.full(TILES, -1, dst.dtype), tiles[:, 0]], 1)
    entry_next = np.concatenate([entry.ravel()[1:], np.full(1, -1, dst.dtype)])

    def by_block(a):
        return a.reshape(EB, EW).T

    arrays = {
        "xt": xp.reshape(NODE_GROUPS, P, NG, KC, P).transpose(0, 4, 3, 2, 1),
        "xrows": xp,
        "et": ep.reshape(EDGE_GROUPS * 2, 2, P, KC, P).transpose(0, 4, 1, 3, 2),
        "slots": np.stack([sp, dp], 1).reshape(EDGE_GROUPS, EG, P, 2).transpose(0, 2, 1, 3),
        "dst_row": dp.reshape(EDGE_GROUPS, EG * P),
        "flag_rows": dp.reshape(EDGE_GROUPS, EG, P).transpose(1, 0, 2).reshape(EG, EDGE_GROUPS * P),
        "cols": np.stack([tiles.T, nxt.T], 1),
        "edge_ends": entry.T,
        "entry_cols": np.stack([by_block(entry.ravel()), by_block(other.ravel()), by_block(entry_next)], 1),
        "entry_row": entry.ravel(),
        "wq": L0_gnn_Wq, "bq": L0_gnn_bq, "wk": L0_gnn_Wk, "bk": L0_gnn_bk, "wv": L0_gnn_Wv, "bv": L0_gnn_bv,
        "we": L0_gnn_We, "ws": L0_gnn_Ws, "bs": L0_gnn_bs,
    }
    arrays = {name: np.ascontiguousarray(a) for name, a in arrays.items()}
    nc = bacc.Bacc("TRN2", target_bir_lowering=False, num_devices=1)
    args = [nc.dram_tensor(f"{name}_dram", a.shape, mybir.dt.from_np(a.dtype), kind="ExternalInput").ap()
            for name, a in arrays.items()]
    out = nc.dram_tensor("out_dram", (NP, D), mybir.dt.from_np(x.dtype), kind="ExternalOutput").ap()
    build(nc, *args, out)
    r = run_bass_kernel_spmd(nc, [{f"{name}_dram": a for name, a in arrays.items()}], core_ids=[0])
    return r.results[0]["out_dram"][:N]
```

```python
from contextlib import ExitStack

import numpy as np

import concourse.bass as bass
from concourse import mybir

P = 128
D = 256
KC = D // P
H = 8
C = D // H
N = 50000
E = 25000

NG = 8
EG = 4
NODE_GROUPS = -(-N // (P * NG))
EDGE_GROUPS = -(-E // (P * EG))
NP = NODE_GROUPS * P * NG
TILES = EDGE_GROUPS * EG
EP = TILES * P
ENTRIES = 2 * TILES
EB = 4
EW = ENTRIES // EB
REC = 2 * D + 2 * H
SKIP = float(1 << 20)
FAR = 1.5e38
EPS = 1e-5
TINY = 1e-16
SCALE = float(C) ** -0.5

assert EDGE_GROUPS % 2 == 1 and NODE_GROUPS % 4 == 1 and ENTRIES % EB == 0 and EW <= P

ALU = mybir.AluOpType
ACT = mybir.ActivationFunctionType
AX = mybir.AxisListType
F32 = mybir.dt.float32
BF16 = mybir.dt.bfloat16
F32R = mybir.dt.float32r
I32 = mybir.dt.int32


def over(eng, sem, value):
    if not (isinstance(value, int) and value <= 0):
        eng.wait_ge(sem, value)


def apart(eng, passed, *waits):
    counts = [v if isinstance(v, int) else eng.lower_val(v) for _, v in waits]
    eng.wait_ge(*passed)
    for (sem, _), value in zip(waits, counts):
        over(eng, sem, value)


def wide(ap, n):
    return ap.unsqueeze(2).to_broadcast([ap.shape[0], ap.shape[1], n])


def build(nc, xt, xrows, et, slots, dst_row, flag_rows, cols, edge_ends, entry_cols, entry_row,
          wq, bq, wk, bk, wv, bv, we, ws, bs, out):
    bounds = nc.dram_tensor("bounds", [ENTRIES, REC], F32)
    with ExitStack() as ctx:
        def sb(name, shape, dt=F32):
            return ctx.enter_context(nc.sbuf_tensor(name, shape, dt))

        def sem(name):
            return ctx.enter_context(nc.semaphore(name))

        bank = [ctx.enter_context(nc.psum_tensor(f"bank{i}", [P, 512], F32)) for i in range(8)]

        ident = sb("ident", [P, P])
        ones = sb("ones", [P, P], BF16)
        half = sb("half", [P, NG])
        w_y = sb("w_y", [P, KC, D])
        w_kv = [sb(f"w_kv{i}", [P, KC, 2 * D], F32R) for i in range(2)]
        w_qs = [sb(f"w_qs{i}", [P, KC, 2 * D], F32R) for i in range(2)]
        w_e = [sb(f"w_e{i}", [P, KC, D], F32R) for i in range(2)]
        bias = sb("bias", [P, 4 * D])
        bias3 = sb("bias3", [P, 4 * D], BF16)
        mean = sb("mean", [P, KC + 1])
        target = sb("target", [EG * H, EDGE_GROUPS, P], I32)
        col_i = sb("col_i", [P, 2, TILES], I32)
        end_i = sb("end_i", [P, 2, TILES], I32)
        col_f = sb("col_f", [P, TILES])
        inner = sb("inner", [P, 3, TILES])
        where = sb("where", [P, TILES], I32)

        xT = [sb(f"xT{p}", [P, KC, NG, P]) for p in range(2)]
        qskv = sb("qskv", [P, 4, EG, 2 * D])
        y = [sb(f"y{p}", [P, NG, D]) for p in range(2)] + [
            qskv[:, 2 + p].rearrange("p j (i d) -> p (j i) d", i=2) for p in range(2)]
        square = [sb(f"square{i}", [P, D]) for i in range(2)]
        ssq = [sb(f"ssq{p}", [P, NG]) for p in range(2)]
        var = [sb(f"var{p}", [P, NG]) for p in range(2)]
        rstd = [sb(f"rstd{p}", [P, NG]) for p in range(2)]

        slot = [sb(f"slot{p}", [P, EG, 2], I32) for p in range(2)]
        goto = [sb(f"goto{p}", [P, EG], I32) for p in range(2)]
        eT = [sb(f"eT{h}", [P, 2 * KC * P]) for h in range(2)]
        e_part = [[sb(f"e_part{i}{h}", [P, 2, KC, P], F32R) for h in range(2)] for i in range(2)]
        dst_all = [sb(f"dst_all{p}", [P, EG * P], I32) for p in range(2)]
        rows_in = [sb(f"rows_in{j}", [P, 2, D]) for j in range(EG)]
        sdT = [[sb(f"sdT{i}{b}", [P, 2, KC, P], F32R) for b in range(2)] for i in range(2)]
        e_sb = [sb(f"e_sb{i}", [P, D]) for i in range(2)]
        qs = [qskv[:, p] for p in range(2)]
        kv = [qskv[:, 2 + p] for p in range(2)]
        prod = sb("prod", [P, D])
        alpha = [sb(f"alpha{p}", [P, EG * H]) for p in range(2)]
        same = [[sb(f"same{p}{j}", [P, P]) for j in range(EG)] for p in range(2)]
        starts = sb("starts", [EG * H, P])
        at = sb("at", [EG * H, P + 1])
        run = sb("run", [EG * H, P])
        peak = sb("peak", [EG * H, P])
        below = sb("below", [P, EG * H])
        mv = sb("mv", [P, EG, D + H])
        dr = [sb(f"dr{p}", [P, EG, 2 * H]) for p in range(2)]
        den = sb("den", [P, EG * H])
        rden = sb("rden", [P, EG * H])
        avgz = sb("avgz", [P, 4, EG, D])
        avg = [avgz[:, p] for p in range(2)]
        z = [avgz[:, 2 + p] for p in range(2)]
        w_raw = avgz[:, 0:2]
        rest = avgz[:, 2].rearrange("p j d -> p (j d)")
        part = [avgz[:, 3].rearrange("p j d -> p (j d)")[:, i * 2 * D:(i + 1) * 2 * D].bitcast(BF16)
                for i in range(2)]
        stats = sb("stats", [P, EG, 6])
        moments = sb("moments", [P, EG, 2])
        vare = sb("vare", [P, EG])
        rstd2 = sb("rstd2", [P, EG])

        rec = sb("rec", [EW, EB, REC])
        ent_i = sb("ent_i", [EW, 3, EB], I32)
        ent_f = sb("ent_f", [EW, EB])
        erow_i = sb("erow_i", [P, ENTRIES], I32)
        eflag = sb("eflag", [H, ENTRIES + 1])
        esame = [xT[1][0:EW].rearrange("p c j n -> p (c j n)")[:, i * ENTRIES:(i + 1) * ENTRIES]
                 for i in range(EB)]
        erun, epeak = (xT[0][0:H].rearrange("p c j n -> p (c j n)")[:, i * ENTRIES:(i + 1) * ENTRIES]
                       for i in range(2))
        ebelow = sb("ebelow", [EW, EB * H])
        ep = sb("ep", [EW, EB * H])
        ekeep = sb("ekeep", [EW, EB])
        emv = y[0][0:EW].rearrange("p j d -> p (j d)")[:, 0:EB * (D + H)].rearrange("p (b w) -> p b w", b=EB)
        egoto = sb("egoto", [EW, EB], I32)
        enext = sb("enext", [EW, EB])
        eden = sb("eden", [EW, EB * H])
        erden = sb("erden", [EW, EB * H])
        ez = y[1][0:EW, 0:EB, :]
        estats = sb("estats", [EW, EB, 6])
        emoments = sb("emoments", [EW, EB, 2])
        evar = sb("evar", [EW, EB])
        erstd = sb("erstd", [EW, EB])

        loaded_y = sem("loaded_y")
        loaded_w = sem("loaded_w")
        loaded_i = sem("loaded_i")
        pool_const = sem("pool_const")
        step = sem("step")
        consts = sem("consts")
        cast = sem("cast")
        left = sem("left")
        x_in = [sem(f"x_in{p}") for p in range(2)]
        node_mm = sem("node_mm")
        biased = sem("biased")
        squared = sem("squared")
        var_ready = sem("var_ready")
        rstd_ready = sem("rstd_ready")
        node_rows = sem("node_rows")
        stored = [sem(f"stored{r}") for r in range(4)]

        slots_in = [sem(f"slots_in{p}") for p in range(2)]
        dst_in = [sem(f"dst_in{p}") for p in range(2)]
        e_in = [sem(f"e_in{h}") for h in range(2)]
        gathered = [sem(f"gathered{j}") for j in range(EG)]
        turned = sem("turned")
        high_ready = sem("high_ready")
        low_ready = sem("low_ready")
        e_high = sem("e_high")
        e_low = sem("e_low")
        prepared = sem("prepared")
        e_mm = sem("e_mm")
        kv_mm = sem("kv_mm")
        qs_mm = sem("qs_mm")
        e_copied = sem("e_copied")
        qs_copied = sem("qs_copied")
        kv_ready = sem("kv_ready")
        prod_ready = sem("prod_ready")
        alpha_ready = sem("alpha_ready")
        same_ready = sem("same_ready")
        alpha_turned = sem("alpha_turned")
        starts_ready = sem("starts_ready")
        flag_ready = sem("flag_ready")
        run_ready = sem("run_ready")
        peak_ready = sem("peak_ready")
        peak_turned = sem("peak_turned")
        below_ready = sem("below_ready")
        peak_kept = sem("peak_kept")
        p_ready = sem("p_ready")
        mv_ready = sem("mv_ready")
        summed = sem("summed")
        den_ready = sem("den_ready")
        den_kept = sem("den_kept")
        rden_ready = sem("rden_ready")
        avg_ready = sem("avg_ready")
        z_ready = sem("z_ready")
        stats_ready = sem("stats_ready")
        moments_ready = sem("moments_ready")
        vare_ready = sem("vare_ready")
        rstd2_ready = sem("rstd2_ready")
        goto_ready = sem("goto_ready")
        edge_rows = sem("edge_rows")
        scattered = [sem(f"scattered{p}") for p in range(2)]
        y_kept = [sem(f"y_kept{p}") for p in range(2)]
        bound_out = [sem(f"bound_out{p}") for p in range(2)]

        rec_in = sem("rec_in")
        t_turned = sem("t_turned")
        t_step = sem("t_step")
        t_p = sem("t_p")
        t_mv = sem("t_mv")
        t_summed = sem("t_summed")
        t_var = sem("t_var")
        t_rstd = sem("t_rstd")
        t_rows = sem("t_rows")
        t_out = sem("t_out")

        turn_b, kv_b, qs_b, e_b, sum_b, small_b = bank[0], bank[1:3], bank[3], bank[4], bank[5:7], bank[7]
        aT_ps = small_b[0:EG * H, 0:P]
        peak_ps = small_b[:, P:P + EG * H]
        den_ps = small_b[:, P + EG * H:P + 2 * EG * H]

        out_groups = out.rearrange("(g p j) d -> g p j d", p=P, j=NG)
        bound_rows = bounds.ap().rearrange("(t r) w -> r t w", r=2)
        NODE_PAIRS = NG // 2
        BOUND_DMAS = 2
        GO_LAST = EDGE_GROUPS - 1

        def groups(eng, body, last, ring):
            for g in range(4):
                body(g, g % ring, g // ring)
            with eng.Fori(0, (last - 4) // ring) as m:
                for k in range(ring):
                    body(m * ring + (4 + k), k, m + 4 // ring)
            body(last, last % ring, last // ring)

        def node_groups(eng, body):
            groups(eng, body, NODE_GROUPS - 1, 4)

        def edge_groups(eng, body):
            groups(eng, body, GO_LAST, 2)

        raw_weights = ((w_qs, D, w_y[:]), (w_kv, 0, w_raw[:, :, 0]), (w_kv, D, w_raw[:, :, 1]),
                       (w_qs, 0, w_raw[:, :, 2]), (w_e, 0, w_raw[:, :, 3]))
        extras = ([[("weights", n)] for n in range(5)] +
                  [[(kind, n)] for n in range(3) for kind in ("biases", "marks")])

        def extra(g, b):
            k = (g - 1) * NODE_PAIRS + b if isinstance(g, int) else -1
            return extras[k] if 0 <= k < len(extras) else []

        def is_first(g):
            return isinstance(g, int) and g == 0

        def is_early(g):
            return isinstance(g, int) and g < 2

        def is_last(g):
            return isinstance(g, int) and g == GO_LAST

        block = ctx.enter_context(nc.Block())

        @block.sync
        def _(sp):
            sp.dma_start(w_y[:], ws.rearrange("(c k) n -> k c n", k=P)).then_inc(loaded_y, 16)
            for i, b in enumerate((bk, bv, bq, bs)):
                sp.dma_start(bias[:, i * D:(i + 1) * D], b.partition_broadcast(P)).then_inc(loaded_y, 16)

            def load_numbers(g, par):
                over(sp, turned, (g - 1) * EG)
                sp.dma_start(slot[par][:], slots[g]).then_inc(slots_in[par], 16)
                over(sp, same_ready, (g - 1) * EG)
                sp.dma_start(dst_all[par][:], dst_row[g].partition_broadcast(P)).then_inc(dst_in[par], 16)

            def load_e(g, h):
                over(sp, e_low, g * 2 + h - 1)
                sp.dma_start(eT[h][:], et[g * 2 + h]).then_inc(e_in[h], 16)

            def load_rest():
                for i, w in enumerate((wk, wv, wq, we)):
                    sp.dma_start(w_raw[:, :, i, :], w.rearrange("(c k) n -> k c n", k=P)).then_inc(loaded_w, 16)
                sp.dma_start(col_i[:], cols).then_inc(loaded_i, 16)
                for i in range(2):
                    sp.dma_start(end_i[:, i, :], edge_ends[i].partition_broadcast(P)).then_inc(loaded_i, 16)
                for j in range(EG):
                    sp.dma_start(target[j * H:(j + 1) * H].rearrange("h g e -> h (g e)"),
                                 flag_rows[j].partition_broadcast(H)).then_inc(loaded_i, 16)
                sp.dma_start(ent_i[:], entry_cols).then_inc(loaded_i, 16)
                sp.dma_start(erow_i[:], entry_row.partition_broadcast(P)).then_inc(loaded_i, 16)
                load_numbers(0, 0)
                load_e(0, 0)
                load_e(0, 1)

            def load_x(g, r, u):
                par = r % 2
                over(sp, node_mm, (g - 1) * NODE_PAIRS)
                sp.dma_start(xT[par][:], xt[g]).then_inc(x_in[par], 16)
                if isinstance(g, int) and g == 1:
                    load_rest()

            node_groups(sp, load_x)

            def keep_y(g, par):
                apart(sp, (x_in[0], 16), (qs_copied, (g + 1) * EG))
                sp.dma_start(bound_rows[:, bass.ds(g * EG, EG), D:2 * D],
                             qs[par][0:P:P - 1, :, D:]).then_inc(y_kept[par], 16)

            def keep_bounds(g, par, u):
                apart(sp, (x_in[0], 16), (avg_ready, g * 2 + 2), (peak_kept, g + 1), (den_kept, g + 1))
                ends = slice(0, P, P - 1)
                table = bound_rows[:, bass.ds(g * EG, EG), :]
                sp.dma_start(table[:, :, 0:D], avg[par][ends]).then_inc(bound_out[par], 16)
                sp.dma_start(table[:, :, 2 * D:], dr[par][ends, :, :]).then_inc(bound_out[par], 16)

            def edge_body(g, par, u):
                if not is_first(g):
                    keep_y(g - 1, 1 - par)
                if not is_last(g):
                    load_numbers(g + 1, 1 - par)
                    load_e(g + 1, 0)
                if not is_early(g):
                    keep_bounds(g - 2, par, u - 1)
                if not is_last(g):
                    load_e(g + 1, 1)

            edge_groups(sp, edge_body)
            keep_y(GO_LAST, 0)
            keep_bounds(GO_LAST - 1, 1, 0)
            keep_bounds(GO_LAST, 0, 0)
            sp.wait_ge(bound_out[0], 16 * BOUND_DMAS * (GO_LAST // 2 + 1))
            sp.wait_ge(bound_out[1], 16 * BOUND_DMAS * (GO_LAST // 2))
            sp.wait_ge(y_kept[0], 16 * (GO_LAST // 2 + 1))
            sp.wait_ge(y_kept[1], 16 * (GO_LAST // 2))
            sp.dma_start(rec[:], bounds.ap().rearrange("(b i) w -> i b w", b=EB)).then_inc(rec_in, 16)
            for r in range(4):
                sp.wait_ge(stored[r], 16 * len(range(r, NODE_GROUPS, 4)))
            sp.wait_ge(scattered[0], 16 * EG * (GO_LAST // 2 + 1))
            sp.wait_ge(scattered[1], 16 * EG * (GO_LAST // 2))
            sp.wait_ge(t_out, 16 * EB)

        @block.gpsimd
        def _(pool):
            nc.gpsimd.memset(ident[:], 0.0).then_inc(pool_const, 1)
            pool.wait_ge(pool_const, 1)
            nc.gpsimd.affine_select(out=ident[:], in_=ident[:], compare_op=ALU.not_equal, fill=1.0, base=0,
                                    pattern=[[-1, P]], channel_multiplier=1).then_inc(pool_const, 1)
            nc.gpsimd.memset(ones[:], 1.0).then_inc(pool_const, 1)
            nc.gpsimd.memset(half[:], -0.5).then_inc(pool_const, 1)
            pool.wait_ge(pool_const, 4)

            def gather(g, par, u, j):
                apart(pool, (pool_const, 4), (turned, (g - 1) * EG + j + 1),
                      *[(slots_in[par], (u + 1) * 16)] * (j == 0))
                for i in range(2):
                    nc.gpsimd.indirect_dma_start(
                        out=rows_in[j][:, i, :], out_offset=None, in_=xrows,
                        in_offset=bass.IndirectOffsetOnAxis(ap=slot[par][:, j, i:i + 1], axis=0),
                    ).then_inc(gathered[j], 16)

            def nodes(g, r, u):
                pool.wait_ge(var_ready, g + 1)
                nc.gpsimd.tensor_tensor(rstd[r % 2][:], var[r % 2][:], half[:], ALU.pow).then_inc(rstd_ready, 1)
                pool.wait_ge(node_rows, g + 1)
                pool.dma_start(out_groups[g], y[r][:]).then_inc(stored[r], 16)
                if isinstance(g, int) and g == 3:
                    for j in range(EG):
                        gather(0, 0, 0, j)

            node_groups(pool, nodes)

            def add_y(g, par, u, b):
                pool.wait_ge(avg_ready, g * 2 + b + 1)
                if b == 0:
                    over(pool, scattered[par], u * 16 * EG)
                for j in (2 * b, 2 * b + 1):
                    ins = nc.gpsimd.tensor_tensor(z[par][:, j, :], avg[par][:, j, :], qs[par][:, j, D:], ALU.add)
                ins.then_inc(z_ready, 1)

            def root(g):
                pool.wait_ge(vare_ready, g + 1)
                nc.gpsimd.tensor_tensor(rstd2[:], vare[:], half[:, 0:EG], ALU.pow).then_inc(rstd2_ready, 1)

            def scatter(g, par, u):
                if is_first(g):
                    for r in range(4):
                        pool.wait_ge(stored[r], 16 * len(range(r, NODE_GROUPS, 4)))
                apart(pool, (pool_const, 4), (edge_rows, g + 1), (goto_ready, g + 1))
                for j in range(EG):
                    nc.gpsimd.indirect_dma_start(
                        out=out, out_offset=bass.IndirectOffsetOnAxis(ap=goto[par][:, j:j + 1], axis=0),
                        in_=z[par][:, j, :], in_offset=None, bounds_check=NP - 1, oob_is_err=False,
                    ).then_inc(scattered[par], 16)

            def finish(g, par, u, more):
                add_y(g, par, u, 0)
                add_y(g, par, u, 1)
                more(0)
                more(1)
                root(g)
                more(2)
                more(3)
                scatter(g, par, u)

            def edge_body(g, par, u):
                def more(j):
                    if not is_last(g):
                        gather(g + 1, 1 - par, u + par, j)
                if is_early(g):
                    for j in range(EG):
                        more(j)
                else:
                    finish(g - 2, par, u - 1, more)

            edge_groups(pool, edge_body)
            finish(GO_LAST - 1, 1, GO_LAST // 2 - 1, lambda j: None)
            finish(GO_LAST, 0, GO_LAST // 2, lambda j: None)

            pool.wait_ge(t_var, 1)
            nc.gpsimd.tensor_tensor(erstd[:], evar[:], half[0:EW, 0:EB], ALU.pow).then_inc(t_rstd, 1)
            pool.wait_ge(t_rows, 1)
            for b in range(EB):
                nc.gpsimd.indirect_dma_start(
                    out=out, out_offset=bass.IndirectOffsetOnAxis(ap=egoto[:, b:b + 1], axis=0),
                    in_=ez[:, b, :], in_offset=None, bounds_check=NP - 1, oob_is_err=False,
                ).then_inc(t_out, 16)

        @block.scalar
        def _(act):
            def cast_weights(n):
                parts, at_col, w = raw_weights[n]
                if n == 1:
                    act.wait_ge(loaded_w, 16 * 4)
                nc.scalar.copy(parts[0][:, :, at_col:at_col + D], w).then_inc(cast, 1)

            def cast_biases(i):
                if i:
                    act.wait_ge(left, i)
                nc.scalar.copy(part[i % 2], rest if i else bias[:]).then_inc(cast, 1)

            def nodes(g, r, u):
                over(act, var_ready, g - 1)
                for b in range(NODE_PAIRS):
                    for kind, n in extra(g, b):
                        if kind == "weights":
                            cast_weights(n)
                        if kind == "biases":
                            cast_biases(n)
                    act.wait_ge(biased, g * NODE_PAIRS + b + 1)
                    for j in (2 * b, 2 * b + 1):
                        over(act, squared, g * NG + j - 1)
                        nc.scalar.activation(square[j % 2][:], y[r][:, j, :], ACT.Square,
                                             accum_out=ssq[r % 2][:, j:j + 1]).then_inc(squared, 1)

            act.wait_ge(consts, 1)
            node_groups(act, nodes)

            def high(g, j):
                t = g * EG + j
                act.wait_ge(turned, t + 1)
                over(act, qs_mm, t - 1)
                nc.scalar.copy(sdT[0][j % 2][:].rearrange("p a c e -> p (a c e)"), turn_b[:]).then_inc(high_ready, 1)

            def high_e(g, h):
                act.wait_ge(e_in[h], (g + 1) * 16)
                over(act, e_mm, (g - 1) * EG + 2 * h + 2)
                nc.scalar.copy(e_part[0][h][:].rearrange("p j c e -> p (j c e)"), eT[h][:]).then_inc(e_high, 1)

            def tile(g, par, u, j):
                t = g * EG + j
                if not (is_last(g) and j == EG - 1):
                    high(g, j + 1) if j < EG - 1 else high(g + 1, 0)
                if j == 1:
                    high_e(g, 1)
                if j == EG - 1 and not is_last(g):
                    high_e(g + 1, 0)
                act.wait_ge(e_mm, t + 1)
                over(act, kv_ready, t - 1)
                nc.scalar.copy(e_sb[j % 2][:], e_b[:, 0:D]).then_inc(e_copied, 1)
                if j == 2 and not is_first(g):
                    weigh(g - 1)
                act.wait_ge(qs_mm, t + 1)
                if j % 2 == 0:
                    over(act, z_ready, (g - 2) * 2 + j // 2 + 1)
                if j == 0:
                    over(act, y_kept[par], u * 16)
                nc.scalar.copy(qs[par][:, j], qs_b[:]).then_inc(qs_copied, 1)

            def weigh(g):
                act.wait_ge(below_ready, g + 1)
                over(act, summed, g)
                nc.scalar.activation(mv[:, :, D:], below[:].rearrange("p (j h) -> p j h", h=H), ACT.Exp,
                                     scale=SCALE).then_inc(p_ready, 1)

            act.wait_ge(squared, NODE_GROUPS * NG)
            high_e(0, 0)
            high(0, 0)

            def edge_body(g, par, u):
                for j in range(EG):
                    tile(g, par, u, j)

            edge_groups(act, edge_body)
            weigh(GO_LAST)
            act.wait_ge(t_step, 4)
            nc.scalar.activation(ep[:], ebelow[:], ACT.Exp, scale=SCALE).then_inc(t_p, 1)

        @block.vector
        def _(dve):
            made = [0]

            def then(ins):
                made[0] += 1
                ins.then_inc(step, 1)
                dve.wait_ge(step, made[0])

            dve.wait_ge(loaded_y, 16 * 5)
            dve.wait_ge(pool_const, 4)
            for c in range(KC):
                diag = w_y[:, c, c * P:(c + 1) * P]
                then(nc.vector.tensor_tensor(diag, diag, ident[:], ALU.add))
            then(nc.vector.tensor_reduce(mean[:, 0:KC], w_y[:], AX.X, ALU.add))
            then(nc.vector.tensor_reduce(mean[:, KC:], bias[:, 3 * D:], AX.X, ALU.add))
            then(nc.vector.tensor_scalar(mean[:], mean[:], 1.0 / D, None, ALU.mult))
            for c in range(KC):
                then(nc.vector.tensor_scalar(w_y[:, c], w_y[:, c], mean[:, c:c + 1], None, ALU.subtract))
            then(nc.vector.tensor_scalar(bias[:, 3 * D:], bias[:, 3 * D:], mean[:, KC:], None, ALU.subtract))
            nc.vector.engine_nop().then_inc(consts, 1)

            def split_weights(n):
                parts, at_col, w = raw_weights[n]
                hi, lo = (a[:, :, at_col:at_col + D] for a in parts)
                dve.wait_ge(cast, n + 1)
                nc.vector.tensor_tensor(lo, w, hi.bitcast(F32), ALU.subtract)

            def split_biases(i):
                dve.wait_ge(cast, len(raw_weights) + i + 1)
                if i < 2:
                    nc.vector.tensor_tensor(rest, rest if i else bias[:], part[i % 2], ALU.subtract).then_inc(left, 1)
                if i == 0:
                    then(nc.vector.tensor_scalar(bias3[:], part[0], ident[:, 0:1], None, ALU.mult))
                else:
                    then(nc.vector.scalar_tensor_tensor(out=bias3[:], in0=part[i % 2], scalar=ident[:, i:i + 1],
                                                        in1=bias3[:], op0=ALU.mult, op1=ALU.add))

            def mark_segments(n):
                if n == 0:
                    dve.wait_ge(loaded_i, 16 * (1 + 2 + EG + 2))
                    nc.vector.memset(at[:, 0:1], -FAR)
                    nc.vector.memset(at[:, P:P + 1], -FAR)
                    nc.vector.tensor_copy(col_f[:], col_i[:, 0, :])
                    nc.vector.tensor_tensor(inner[:, 0, :], col_i[:, 0, :], col_i[:, 1, :], ALU.is_equal)
                if n == 1:
                    nc.vector.tensor_tensor(inner[:, 1, :], col_i[:, 0, :], end_i[:, 0, :], ALU.is_equal)
                    then(nc.vector.tensor_tensor(inner[:, 2, :], col_i[:, 0, :], end_i[:, 1, :], ALU.is_equal))
                if n == 2:
                    then(nc.vector.tensor_tensor(inner[:, 0, :], inner[:, 0, :], inner[:, 1, :], ALU.max))
                    then(nc.vector.tensor_tensor(inner[:, 0, :], inner[:, 0, :], inner[:, 2, :], ALU.max))
                    then(nc.vector.scalar_tensor_tensor(out=where[:], in0=inner[:, 0, :], scalar=SKIP, in1=col_f[:],
                                                        op0=ALU.mult, op1=ALU.add))
                    nc.vector.engine_nop().then_inc(prepared, 1)

            def add_bias(g, r, u, b):
                if b == 0:
                    over(dve, stored[r], u * 16)
                dve.wait_ge(node_mm, g * NODE_PAIRS + b + 1)
                nc.vector.tensor_tensor(
                    y[r][:, 2 * b:2 * b + 2, :],
                    bank[r % 2 * NODE_PAIRS + b][:].rearrange("p (j d) -> p j d", j=2),
                    bias[:, 3 * D:].unsqueeze(1).to_broadcast([P, 2, D]), ALU.add).then_inc(biased, 1)

            def variance(g, r):
                dve.wait_ge(squared, (g + 1) * NG)
                over(dve, rstd_ready, g - 1)
                nc.vector.tensor_scalar(var[r % 2][:], ssq[r % 2][:], 1.0 / D, EPS, ALU.mult,
                                        ALU.add).then_inc(var_ready, 1)

            def scale(g, r, tiles):
                if tiles[0] == 0:
                    dve.wait_ge(rstd_ready, g + 1)
                for j in tiles:
                    ins = nc.vector.tensor_scalar(y[r][:, j, :], y[r][:, j, :], rstd[r % 2][:, j:j + 1],
                                                  None, ALU.mult)
                if tiles[-1] == NG - 1:
                    ins.then_inc(node_rows, 1)

            def nodes(g, r, u):
                steps = (lambda: variance(g - 1, (r - 1) % 4),
                         lambda: scale(g - 1, (r - 1) % 4, range(NG // 2)),
                         lambda: scale(g - 1, (r - 1) % 4, range(NG // 2, NG)), lambda: None)
                for b in range(NODE_PAIRS):
                    add_bias(g, r, u, b)
                    for kind, n in extra(g, b):
                        {"weights": split_weights, "biases": split_biases, "marks": mark_segments}[kind](n)
                    if not is_first(g):
                        steps[b]()

            node_groups(dve, nodes)
            variance(NODE_GROUPS - 1, 0)
            scale(NODE_GROUPS - 1, 0, range(NG))
            for r in (2, 3):
                dve.wait_ge(stored[r], 16 * (NODE_GROUPS // 4))

            def low(g, j):
                t = g * EG + j
                dve.wait_ge(high_ready, t + 1)
                nc.vector.tensor_tensor(sdT[1][j % 2][:].rearrange("p a c e -> p (a c e)"), turn_b[:],
                                        sdT[0][j % 2][:].rearrange("p a c e -> p (a c e)").bitcast(F32),
                                        ALU.subtract).then_inc(low_ready, 1)

            def low_e(g, h):
                dve.wait_ge(e_high, g * 2 + h + 1)
                nc.vector.tensor_tensor(e_part[1][h][:].rearrange("p j c e -> p (j c e)"), eT[h][:],
                                        e_part[0][h][:].rearrange("p j c e -> p (j c e)").bitcast(F32),
                                        ALU.subtract).then_inc(e_low, 1)

            def tile(g, par, u, j):
                t = g * EG + j
                if not (is_last(g) and j == EG - 1):
                    low(g, j + 1) if j < EG - 1 else low(g + 1, 0)
                if j == 1:
                    low_e(g, 1)
                if j == EG - 1 and not is_last(g):
                    low_e(g + 1, 0)
                dve.wait_ge(kv_mm, t + 1)
                dve.wait_ge(e_copied, t + 1)
                if j == 0:
                    over(dve, mv_ready, g - 1)
                nc.vector.tensor_tensor(kv[par][:, j].rearrange("p (a d) -> p a d", a=2),
                                        kv_b[j % 2][:].rearrange("p (a d) -> p a d", a=2),
                                        e_sb[j % 2][:].unsqueeze(1).to_broadcast([P, 2, D]),
                                        ALU.add).then_inc(kv_ready, 1)
                if j == 0:
                    dve.wait_ge(dst_in[par], (u + 1) * 16)
                    over(dve, summed, g - 1)
                nc.vector.tensor_scalar(same[par][j][:], dst_all[par][:, j * P:(j + 1) * P],
                                        col_f[:, bass.ds(t, 1)], None, ALU.is_equal).then_inc(same_ready, 1)
                dve.wait_ge(qs_copied, t + 1)
                dve.wait_ge(kv_ready, t + 1)
                over(dve, alpha_ready, t)
                nc.vector.tensor_tensor(prod[:], kv[par][:, j, 0:D], qs[par][:, j, 0:D],
                                        ALU.mult).then_inc(prod_ready, 1)
                dve.wait_ge(prod_ready, t + 1)
                if j == 0:
                    over(dve, alpha_turned, g - 1)
                    over(dve, below_ready, g - 1)
                nc.vector.tensor_reduce(alpha[par][:, j * H:(j + 1) * H],
                                        prod[:].rearrange("p (h c) -> p h c", h=H), AX.X,
                                        ALU.add).then_inc(alpha_ready, 1)

            def maxima(g):
                over(dve, peak_ready, g)
                group = target[:, bass.ds(g, 1), :].rearrange("p o e -> p (o e)")
                nc.vector.tensor_tensor(starts[:, 1:], group[:, 1:], group[:, 0:P - 1],
                                        ALU.not_equal).then_inc(starts_ready, 1)
                dve.wait_ge(starts_ready, g + 1)
                nc.vector.tensor_scalar(at[:, 1:P], starts[:, 1:], -FAR, None, ALU.mult).then_inc(flag_ready, 1)
                dve.wait_ge(flag_ready, g + 1)
                dve.wait_ge(alpha_turned, g + 1)
                nc.vector.tensor_tensor_scan(run[:], at[:, 0:P], aT_ps, -FAR, ALU.add, ALU.max).then_inc(run_ready, 1)
                dve.wait_ge(run_ready, g + 1)
                over(dve, peak_turned, g)
                nc.vector.tensor_tensor_scan(peak[:, ::-1], at[:, 1:P + 1][:, ::-1], run[:, ::-1], -FAR,
                                             ALU.add, ALU.max).then_inc(peak_ready, 1)

            def shift(g, par, u):
                dve.wait_ge(peak_turned, g + 1)
                over(dve, p_ready, g)
                nc.vector.tensor_tensor(below[:], alpha[par][:], peak_ps, ALU.subtract).then_inc(below_ready, 1)
                over(dve, bound_out[par], u * 16 * BOUND_DMAS)
                nc.vector.tensor_copy(dr[par][:, :, H:], peak_ps.rearrange("p (j h) -> p j h", h=H)).then_inc(peak_kept, 1)

            def weigh(g, par):
                dve.wait_ge(p_ready, g + 1)
                over(dve, summed, g)
                for j in range(EG):
                    ins = nc.vector.tensor_tensor(
                        mv[:, j, 0:D].rearrange("p (h c) -> p h c", h=H),
                        kv[par][:, j, D:].rearrange("p (h c) -> p h c", h=H),
                        wide(mv[:, j, D:], C), ALU.mult)
                ins.then_inc(mv_ready, 1)

            def average(g, par, u):
                dve.wait_ge(summed, g + 1)
                over(dve, rden_ready, g)
                nc.vector.tensor_scalar(den[:], den_ps, TINY, None, ALU.add).then_inc(den_ready, 1)
                nc.vector.tensor_copy(dr[par][:, :, 0:H], den_ps.rearrange("p (j h) -> p j h", h=H)).then_inc(den_kept, 1)
                dve.wait_ge(den_ready, g + 1)
                over(dve, avg_ready, g * 2)
                nc.vector.reciprocal(rden[:], den[:]).then_inc(rden_ready, 1)
                dve.wait_ge(rden_ready, g + 1)
                over(dve, bound_out[par], u * 16 * BOUND_DMAS)
                for b in range(2):
                    nc.vector.tensor_tensor(
                        avg[par][:, 2 * b:2 * b + 2, :].rearrange("p j (h c) -> p (j h) c", h=H),
                        sum_b[b][:].rearrange("p (h c) -> p h c", c=C),
                        wide(rden[:, 2 * b * H:(2 * b + 2) * H], C), ALU.mult).then_inc(avg_ready, 1)

            def spread(g, par):
                dve.wait_ge(z_ready, g * 2 + 2)
                over(dve, moments_ready, g)
                for j in range(EG):
                    ins = nc.vector.bn_stats(stats[:, j, :], z[par][:, j, :])
                ins.then_inc(stats_ready, 1)
                apart(dve, (pool_const, 4), (stats_ready, g + 1), (edge_rows, g))
                for j in range(EG):
                    ins = nc.vector.bn_aggr(moments[:, j, :], stats[:, j, :])
                ins.then_inc(moments_ready, 1)
                dve.wait_ge(moments_ready, g + 1)
                over(dve, rstd2_ready, g)
                nc.vector.tensor_scalar(vare[:], moments[:, :, 1], EPS, None, ALU.add).then_inc(vare_ready, 1)

            def rows(g, par, u):
                over(dve, scattered[par], u * 16 * EG)
                nc.vector.tensor_copy(goto[par][:], where[:, bass.ds(g * EG, EG)]).then_inc(goto_ready, 1)
                dve.wait_ge(rstd2_ready, g + 1)
                for j in range(EG):
                    ins = nc.vector.tensor_scalar(z[par][:, j, :], z[par][:, j, :], moments[:, j, 0:1],
                                                  rstd2[:, j:j + 1], ALU.subtract, ALU.mult)
                ins.then_inc(edge_rows, 1)

            low_e(0, 0)
            low(0, 0)

            def edge_body(g, par, u):
                if not is_early(g):
                    average(g - 2, par, u - 1)
                tile(g, par, u, 0)
                if not is_first(g):
                    maxima(g - 1)
                tile(g, par, u, 1)
                if not is_first(g):
                    shift(g - 1, 1 - par, u - 1 + par)
                if not is_early(g):
                    spread(g - 2, par)
                tile(g, par, u, 2)
                if not is_first(g):
                    weigh(g - 1, 1 - par)
                if not is_early(g):
                    rows(g - 2, par, u - 1)
                tile(g, par, u, 3)

            edge_groups(dve, edge_body)
            last_u = GO_LAST // 2
            average(GO_LAST - 1, 1, last_u - 1)
            maxima(GO_LAST)
            shift(GO_LAST, 0, last_u)
            weigh(GO_LAST, 0)
            spread(GO_LAST - 1, 1)
            rows(GO_LAST - 1, 1, last_u - 1)
            average(GO_LAST, 0, last_u)
            spread(GO_LAST, 0)
            rows(GO_LAST, 0, last_u)

            t_made = [0]

            def t_then(ins):
                t_made[0] += 1
                ins.then_inc(t_step, 1)
                dve.wait_ge(t_step, t_made[0])

            nc.vector.memset(eflag[:, 0:1], -FAR)
            nc.vector.memset(eflag[:, ENTRIES:], -FAR)
            then(nc.vector.tensor_tensor(eflag[:, 1:ENTRIES], erow_i[0:H, 1:], erow_i[0:H, 0:ENTRIES - 1], ALU.not_equal))
            then(nc.vector.tensor_scalar(eflag[:, 1:ENTRIES], eflag[:, 1:ENTRIES], -FAR, None, ALU.mult))
            then(nc.vector.tensor_copy(ent_f[:], ent_i[:, 0, :]))
            then(nc.vector.tensor_tensor(ekeep[:], ent_i[:, 0, :], ent_i[:, 1, :], ALU.not_equal))
            then(nc.vector.tensor_tensor(enext[:], ent_i[:, 0, :], ent_i[:, 2, :], ALU.is_equal))
            then(nc.vector.scalar_tensor_tensor(out=egoto[:], in0=enext[:], scalar=SKIP, in1=ent_f[:],
                                                op0=ALU.mult, op1=ALU.add))
            for i in range(EB):
                ins = nc.vector.tensor_scalar(esame[i], erow_i[0:EW, :], ent_f[:, i:i + 1], None, ALU.is_equal)
            then(ins)
            dve.wait_ge(t_turned, 1)
            t_then(nc.vector.tensor_tensor_scan(erun, eflag[:, 0:ENTRIES], kv_b[0][0:H, 0:ENTRIES], -FAR,
                                                ALU.add, ALU.max))
            t_then(nc.vector.tensor_tensor_scan(epeak[:, ::-1], eflag[:, 1:][:, ::-1], erun[:, ::-1], -FAR,
                                                ALU.add, ALU.max))
            dve.wait_ge(t_turned, 2)
            dve.wait_ge(rec_in, 16)
            t_then(nc.vector.tensor_tensor(ebelow[:].rearrange("p (b h) -> p b h", h=H), rec[:, :, 2 * D + H:],
                                           kv_b[1][0:EW, 0:EB * H].rearrange("p (b h) -> p b h", h=H), ALU.subtract))
            t_then(nc.vector.tensor_tensor(emv[:, :, D:], rec[:, :, 2 * D:2 * D + H], wide(ekeep[:], H), ALU.mult))
            dve.wait_ge(t_p, 1)
            t_then(nc.vector.tensor_tensor(emv[:, :, D:], emv[:, :, D:], ep[:].rearrange("p (b h) -> p b h", h=H), ALU.mult))
            for b in range(EB):
                ins = nc.vector.tensor_tensor(emv[:, b, 0:D].rearrange("p (h c) -> p h c", h=H),
                                              rec[:, b, 0:D].rearrange("p (h c) -> p h c", h=H),
                                              wide(emv[:, b, D:], C), ALU.mult)
            ins.then_inc(t_mv, 1)
            for b in range(EB):
                dve.wait_ge(t_summed, b + 1)
                t_then(nc.vector.tensor_scalar(eden[:, b * H:(b + 1) * H], bank[3 + b][0:EW, D:D + H], TINY, None, ALU.add))
                t_then(nc.vector.reciprocal(erden[:, b * H:(b + 1) * H], eden[:, b * H:(b + 1) * H]))
                t_then(nc.vector.tensor_tensor(ez[:, b, :].rearrange("p (h c) -> p h c", h=H),
                                               bank[3 + b][0:EW, 0:D].rearrange("p (h c) -> p h c", h=H),
                                               wide(erden[:, b * H:(b + 1) * H], C), ALU.mult))
                t_then(nc.vector.tensor_tensor(ez[:, b, :], ez[:, b, :], rec[:, b, D:2 * D], ALU.add))
                t_then(nc.vector.bn_stats(estats[:, b, :], ez[:, b, :]))
                t_then(nc.vector.bn_aggr(emoments[:, b, :], estats[:, b, :]))
            nc.vector.tensor_scalar(evar[:], emoments[:, :, 1], EPS, None, ALU.add).then_inc(t_var, 1)
            dve.wait_ge(t_rstd, 1)
            for b in range(EB):
                ins = nc.vector.tensor_scalar(ez[:, b, :], ez[:, b, :], emoments[:, b, 0:1], erstd[:, b:b + 1],
                                              ALU.subtract, ALU.mult)
            ins.then_inc(t_rows, 1)

        @block.tensor
        def _(pe):
            pe.wait_ge(consts, 1)

            def nodes(g, r, u):
                par = r % 2
                pe.wait_ge(x_in[par], (u * 2 + (r // 2 + 1)) * 16)
                for b in range(NODE_PAIRS):
                    over(pe, biased, (g - 2) * NODE_PAIRS + b + 1)
                    for i in range(2):
                        for c in range(KC):
                            ins = nc.tensor.matmul(bank[par * NODE_PAIRS + b][:, i * D:(i + 1) * D],
                                                   xT[par][:, c, 2 * b + i, :], w_y[:, c, :],
                                                   start=(c == 0), stop=(c == KC - 1))
                    ins.then_inc(node_mm, 1)

            node_groups(pe, nodes)
            pe.wait_ge(biased, NODE_GROUPS * NODE_PAIRS)

            def turn(g, j):
                t = g * EG + j
                pe.wait_ge(gathered[j], (g + 1) * 32)
                over(pe, low_ready, t)
                for i in range(2):
                    for c in range(KC):
                        ins = nc.tensor.transpose(turn_b[:, (i * KC + c) * P:(i * KC + c + 1) * P],
                                                  rows_in[j][:, i, c * P:(c + 1) * P], ident[:])
                ins.then_inc(turned, 1)

            def product(to, rows, weights, first):
                terms = [(c, a, b) for c in range(KC) for a, b in ((0, 0), (0, 1), (1, 0))]
                for n, (c, a, b) in enumerate(terms):
                    ins = nc.tensor.matmul(to, rows[a][:, c, :], weights[b][:, c, :],
                                           start=(first and n == 0), stop=(n == len(terms) - 1))
                return ins

            def tile(g, par, u, j):
                t = g * EG + j
                if not (is_last(g) and j == EG - 1):
                    turn(g, j + 1) if j < EG - 1 else turn(g + 1, 0)
                if j % 2 == 0:
                    pe.wait_ge(e_low, g * 2 + j // 2 + 1)
                over(pe, e_copied, t)
                product(e_b[:, 0:D], [a[j // 2][:, j % 2] for a in e_part], w_e, True).then_inc(e_mm, 1)
                pe.wait_ge(low_ready, t + 1)
                over(pe, kv_ready, t - 1)
                nc.tensor.matmul(kv_b[j % 2][:], ones[:], bias3[:, 0:2 * D], start=True, stop=False)
                product(kv_b[j % 2][:], [a[j % 2][:, 0] for a in sdT], w_kv, False).then_inc(kv_mm, 1)
                over(pe, qs_copied, t)
                nc.tensor.matmul(qs_b[:], ones[:], bias3[:, 2 * D:], start=True, stop=False)
                product(qs_b[:], [a[j % 2][:, 1] for a in sdT], w_qs, False).then_inc(qs_mm, 1)

            def turn_alpha(g, par):
                pe.wait_ge(alpha_ready, (g + 1) * EG)
                over(pe, den_kept, g)
                nc.tensor.transpose(aT_ps, alpha[par][:], ident[:]).then_inc(alpha_turned, 1)

            def turn_peak(g):
                apart(pe, (consts, 1), (peak_ready, g + 1))
                nc.tensor.transpose(peak_ps, peak[:], ident[0:EG * H, 0:EG * H]).then_inc(peak_turned, 1)

            def add_up(g, par):
                pe.wait_ge(mv_ready, g + 1)
                pe.wait_ge(peak_kept, g + 1)
                pe.wait_ge(same_ready, (g + 1) * EG)
                over(pe, avg_ready, g * 2)
                for j in range(EG):
                    nc.tensor.matmul(sum_b[j // 2][:, (j % 2) * D:(j % 2 + 1) * D], same[par][j][:],
                                     mv[:, j, 0:D], start=True, stop=True)
                    ins = nc.tensor.matmul(den_ps[:, j * H:(j + 1) * H], same[par][j][:], mv[:, j, D:],
                                           start=True, stop=True)
                ins.then_inc(summed, 1)

            pe.wait_ge(prepared, 1)
            turn(0, 0)

            def edge_body(g, par, u):
                tile(g, par, u, 0)
                if not is_first(g):
                    turn_alpha(g - 1, 1 - par)
                tile(g, par, u, 1)
                if not is_first(g):
                    turn_peak(g - 1)
                tile(g, par, u, 2)
                tile(g, par, u, 3)
                if not is_first(g):
                    add_up(g - 1, 1 - par)

            edge_groups(pe, edge_body)
            turn_alpha(GO_LAST, 0)
            turn_peak(GO_LAST)
            add_up(GO_LAST, 0)

            pe.wait_ge(rec_in, 16)
            for b in range(EB):
                ins = nc.tensor.transpose(kv_b[0][0:H, b * EW:(b + 1) * EW], rec[:, b, 2 * D + H:],
                                          ident[0:EW, 0:EW])
            ins.then_inc(t_turned, 1)
            pe.wait_ge(t_step, 2)
            for b in range(EB):
                ins = nc.tensor.transpose(kv_b[1][0:EW, b * H:(b + 1) * H], epeak[:, b * EW:(b + 1) * EW],
                                          ident[0:H, 0:H])
            ins.then_inc(t_turned, 1)
            pe.wait_ge(t_mv, 1)
            pe.wait_ge(avg_ready, 2 * EDGE_GROUPS)
            for b in range(EB):
                for i in range(EB):
                    ins = nc.tensor.matmul(bank[3 + b][0:EW, 0:D + H], esame[i][:, b * EW:(b + 1) * EW],
                                           emv[:, i, :], start=(i == 0), stop=(i == EB - 1))
                ins.then_inc(t_summed, 1)

    return nc


def kernel(x, src, dst, edge_attr_256, L0_gnn_Wq, L0_gnn_bq, L0_gnn_Wk, L0_gnn_bk, L0_gnn_Wv, L0_gnn_bv,
           L0_gnn_We, L0_gnn_Ws, L0_gnn_bs):
    import concourse.bacc as bacc
    from concourse.bass_utils import run_bass_kernel_spmd

    x, src, dst, ea = (np.asarray(a) for a in (x, src, dst, edge_attr_256))
    xp = np.zeros((NP, D), x.dtype)
    xp[:N] = x
    ep = np.zeros((EP, D), ea.dtype)
    ep[:E] = ea
    sp = np.zeros(EP, src.dtype)
    sp[:E] = src
    dp = np.full(EP, N, dst.dtype)
    dp[:E] = dst

    tiles = dp.reshape(TILES, P)
    nxt = np.concatenate([dp[1:], dp[-1:]]).reshape(TILES, P)
    entry = tiles[:, [0, P - 1]]
    other = np.stack([np.full(TILES, -1, dst.dtype), tiles[:, 0]], 1)
    entry_next = np.concatenate([entry.ravel()[1:], np.full(1, -1, dst.dtype)])

    def by_block(a):
        return a.reshape(EB, EW).T

    arrays = {
        "xt": xp.reshape(NODE_GROUPS, P, NG, KC, P).transpose(0, 4, 3, 2, 1),
        "xrows": xp,
        "et": ep.reshape(EDGE_GROUPS * 2, 2, P, KC, P).transpose(0, 4, 1, 3, 2),
        "slots": np.stack([sp, dp], 1).reshape(EDGE_GROUPS, EG, P, 2).transpose(0, 2, 1, 3),
        "dst_row": dp.reshape(EDGE_GROUPS, EG * P),
        "flag_rows": dp.reshape(EDGE_GROUPS, EG, P).transpose(1, 0, 2).reshape(EG, EDGE_GROUPS * P),
        "cols": np.stack([tiles.T, nxt.T], 1),
        "edge_ends": entry.T,
        "entry_cols": np.stack([by_block(entry.ravel()), by_block(other.ravel()), by_block(entry_next)], 1),
        "entry_row": entry.ravel(),
        "wq": L0_gnn_Wq, "bq": L0_gnn_bq, "wk": L0_gnn_Wk, "bk": L0_gnn_bk, "wv": L0_gnn_Wv, "bv": L0_gnn_bv,
        "we": L0_gnn_We, "ws": L0_gnn_Ws, "bs": L0_gnn_bs,
    }
    arrays = {name: np.ascontiguousarray(a) for name, a in arrays.items()}
    nc = bacc.Bacc("TRN2", target_bir_lowering=False, num_devices=1)
    args = [nc.dram_tensor(f"{name}_dram", a.shape, mybir.dt.from_np(a.dtype), kind="ExternalInput").ap()
            for name, a in arrays.items()]
    out = nc.dram_tensor("out_dram", (NP, D), mybir.dt.from_np(x.dtype), kind="ExternalOutput").ap()
    build(nc, *args, out)
    r = run_bass_kernel_spmd(nc, [{f"{name}_dram": a for name, a in arrays.items()}], core_ids=[0])
    return r.results[0]["out_dram"][:N]
```
